# Optimizing a Trainium2 kernel written in Bass

```python
import numpy as np
import jax
import jax.numpy as jnp

def _softmax(x, axis=-1):
    return jax.nn.softmax(x, axis=axis)

def _gelu(x):
    return jax.nn.gelu(x, approximate=True)

def _silu(x):
    return jax.nn.silu(x)

def _sigmoid(x):
    return jax.nn.sigmoid(x)

def _layernorm(x, axis=-1, eps=1e-05):
    m = jnp.mean(x, axis=axis, keepdims=True)
    v = jnp.var(x, axis=axis, keepdims=True)
    return (x - m) / jnp.sqrt(v + eps)

def _scatter_add(tgt, idx, src, axis=0):
    return tgt.at[idx].add(src)

def _segment_sum(src, seg, n):
    return jax.ops.segment_sum(src, seg, n)
kernel_name = 'mk_rec_standalone_d1_rec_r8_6bdfae'

def setup_inputs(seed: int=0):
    np.random.seed(seed)
    _w = jnp.asarray

    def _rec_inputs():
        import jax
        import jax.numpy as jnp
        _rk = jax.random.key(seed)
        r_M = -0.00340659 + 1.00146 * jax.random.normal(jax.random.fold_in(_rk, 1), (512, 512), jnp.float32)
        r_mask = jax.random.bernoulli(jax.random.fold_in(_rk, 2), 0.8999, (1, 512, 6250))
        return (r_M, r_mask)
    r_M, r_mask = _rec_inputs()

    def _L0_rec_setup():
        import jax, jax.numpy as jnp
        import numpy as np
        HEADS = 8
        DIM_HEADS = 64
        LN_EPS = 1e-05

        def layer_norm(x):
            mu = jnp.mean(x, axis=-1, keepdims=True)
            var = jnp.var(x, axis=-1, keepdims=True)
            return (x - mu) / jnp.sqrt(var + LN_EPS)
        key = jax.random.key(seed)
        ks = jax.random.split(key, 12)
        e, n, M_dim, d = (256, 6250, 512, 256)
        inner = HEADS * DIM_HEADS
        s = lambda fan: 1.0 / np.sqrt(fan)
        return {'M': jax.random.normal(ks[0], (e, M_dim), jnp.float32), 'x': jax.random.normal(ks[1], (n, d), jnp.float32), 'mask': jax.random.bernoulli(ks[2], 0.9, (1, e, n)), 'Wq': jax.random.normal(ks[3], (inner, M_dim), jnp.float32) * s(M_dim), 'Wkv': jax.random.normal(ks[4], (2 * inner, d), jnp.float32) * s(d), 'bkv': jax.random.normal(ks[5], (2 * inner,), jnp.float32) * 0.01, 'Wo': jax.random.normal(ks[6], (M_dim, inner), jnp.float32) * s(inner), 'bo': jax.random.normal(ks[7], (M_dim,), jnp.float32) * 0.01, 'W1': jax.random.normal(ks[8], (4 * M_dim, M_dim), jnp.float32) * s(M_dim), 'b1': jax.random.normal(ks[9], (4 * M_dim,), jnp.float32) * 0.01, 'W2': jax.random.normal(ks[10], (M_dim, 4 * M_dim), jnp.float32) * s(4 * M_dim), 'b2': jax.random.normal(ks[11], (M_dim,), jnp.float32) * 0.01}
    _L0_rec_all = _L0_rec_setup()
    _L0_rec_in = {k: v for k, v in _L0_rec_all.items() if k in ('x', 'Wq', 'Wkv', 'bkv', 'Wo', 'bo', 'W1', 'b1', 'W2', 'b2')}
    del _L0_rec_all
    return {'r_M': r_M, 'r_mask': r_mask, 'L0_rec_x': _L0_rec_in['x'], 'L0_rec_Wq': _L0_rec_in['Wq'], 'L0_rec_Wkv': _L0_rec_in['Wkv'], 'L0_rec_bkv': _L0_rec_in['bkv'], 'L0_rec_Wo': _L0_rec_in['Wo'], 'L0_rec_bo': _L0_rec_in['bo'], 'L0_rec_W1': _L0_rec_in['W1'], 'L0_rec_b1': _L0_rec_in['b1'], 'L0_rec_W2': _L0_rec_in['W2'], 'L0_rec_b2': _L0_rec_in['b2']}

def reference(r_M, r_mask, L0_rec_x, L0_rec_Wq, L0_rec_Wkv, L0_rec_bkv, L0_rec_Wo, L0_rec_bo, L0_rec_W1, L0_rec_b1, L0_rec_W2, L0_rec_b2):
    import jax
    import jax.numpy as jnp

    def _L0_rec_ref(M, x, mask, Wq, Wkv, bkv, Wo, bo, W1, b1, W2, b2):
        import jax, jax.numpy as jnp
        import numpy as np
        HEADS = 8
        DIM_HEADS = 64
        LN_EPS = 1e-05

        def layer_norm(x):
            mu = jnp.mean(x, axis=-1, keepdims=True)
            var = jnp.var(x, axis=-1, keepdims=True)
            return (x - mu) / jnp.sqrt(var + LN_EPS)
        e, M_dim = M.shape
        h, dh = (HEADS, DIM_HEADS)
        q = (M @ Wq.T).reshape(e, h, dh).transpose(1, 0, 2)
        kv = x @ Wkv.T + bkv
        k, v = jnp.split(kv, 2, axis=-1)
        n = x.shape[0]
        k = k.reshape(n, h, dh).transpose(1, 0, 2)
        v = v.reshape(n, h, dh).transpose(1, 0, 2)
        sim = jnp.einsum('hid,hjd->hij', q, k) * dh ** (-0.5)
        sim = jnp.where(mask, sim, -1000000000.0)
        attn = jax.nn.softmax(sim, axis=-1)
        out = jnp.einsum('hij,hjd->hid', attn, v)
        out = out.transpose(1, 0, 2).reshape(e, h * dh)
        out = out @ Wo.T + bo
        m = layer_norm(out + M)
        ffn = jax.nn.relu(m @ W1.T + b1) @ W2.T + b2
        z = layer_norm(ffn + m)
        return z
    y = _L0_rec_ref(r_M, L0_rec_x, r_mask, L0_rec_Wq, L0_rec_Wkv, L0_rec_bkv, L0_rec_Wo, L0_rec_bo, L0_rec_W1, L0_rec_b1, L0_rec_W2, L0_rec_b2)
    return y

_drawn_inputs = setup_inputs


def setup_inputs(seed=0):
    import zlib

    import numpy as np

    out = dict(_drawn_inputs(seed))
    spreads = {}
    factors = {'L0_rec_bkv': 5.271, 'L0_rec_bo': 5.614, 'L0_rec_b1': 8.0, 'L0_rec_b2': 6.723}
    for name, (base, spread) in spreads.items():
        noise = np.random.default_rng([zlib.crc32(name.encode()), seed]).standard_normal(out[name].shape)
        drawn = base * np.exp(spread * noise) if base else spread * noise
        out[name] = jnp.asarray(drawn.astype(out[name].dtype))
    for name, factor in factors.items():
        out[name] = (out[name] * factor).astype(out[name].dtype)
    return out
```

```python
from contextlib import ExitStack

import concourse.bass as bass
from concourse import mybir
from concourse.alu_op_type import AluOpType as ALU

ACT = mybir.ActivationFunctionType
F32 = mybir.dt.float32
F32R = mybir.dt.float32r
BF16 = mybir.dt.bfloat16
U8 = mybir.dt.uint8

P = 128
E = 512
N = 6250
D = 256
DM = 512
INNER = 512
HEADS = 8
DH = 64
FF = 2048
QT = E // P
PAIRS = HEADS // 2
U = 2 * QT
KT = 7
CHUNK = KT * P
CHUNKS = -(-N // CHUNK)
NPAD = CHUNKS * CHUNK
HALF = CHUNK // 2
TV = 2 * KT
FT = FF // P
DC = D // P
MC = DM // P
BIG = 2.0 ** 100
EPS = 1e-5
HALVES = [(half, to) for half in range(2) for to in range(2)]
SCALE = DH ** -0.5

TERMS = ((0, 0), (0, 1), (1, 0))

Q_SLOTS = PAIRS
V_SLOTS = -(-KT // 2)
PRE = Q_SLOTS + PAIRS
BODY = PAIRS * U + V_SLOTS + PAIRS


def chunk_schedule(first, last):
    out = []

    def weave(p, k, tv):
        out.extend([("S", p, 0), ("S", p, 1), ("E", p, 0)])
        if p >= 1:
            out.append(("Z", p - 1, 0))
        done = 2
        if p == 0:
            if not first:
                out.append(("C", -1, 0))
            for v in range(V_SLOTS):
                out.append(("V", 0, v))
                if v == 0 and not first:
                    out.extend([("F", -1, 0), ("A", -1, 0)])
                for _ in range(2):
                    if done < U:
                        out.extend([("S", p, done), ("E", p, done - 1)])
                        done += 1
        else:
            if p >= 2:
                out.append(("C", p - 2, 0))
            if p == 1 and not last:
                out.append(("X", 0, 0))
            out.extend([("T", tv, 0), ("T", tv, 1)])
            if p >= 2:
                out.extend([("F", p - 2, 0), ("A", p - 2, 0)])
            for n in range(TV):
                if n + 2 < TV:
                    out.append(("T", tv, n + 2))
                out.append(("W", tv, n))
                while done < U and (done - 1) * TV <= (n + 1) * (U - 1):
                    out.extend([("S", p, done), ("E", p, done - 1)])
                    done += 1
        while done < U:
            out.extend([("S", p, done), ("E", p, done - 1)])
            done += 1
        out.append(("E", p, U - 1))

    for p in range(PAIRS):
        weave(p, 0, p - 1)
    tail = PAIRS - 1
    if not last:
        out.extend([("K", 0, 0)])
    out.extend([("C", tail - 1, 0), ("Z", tail, 0)])
    if not last:
        out.extend([("K", 1, 0), ("K", 2, 0)])
    out.extend([("F", tail - 1, 0), ("A", tail - 1, 0)])
    if not last:
        out.extend([("K", 3, 0)])
    out.extend([("T", tail, 0), ("T", tail, 1)])
    for n in range(TV):
        if n + 2 < TV:
            out.append(("T", tail, n + 2))
        out.append(("W", tail, n))
    if last:
        out.extend([("C", tail, 0), ("F", tail, 0), ("A", tail, 0)])
    return out


def build(nc, x, mask, mt, mn, wq, wk, wv, bk, bv, wo, bo, w1, b1, w2, b2, out):
    with ExitStack() as ctx:
        def sb(name, shape, dt, where=ctx):
            return where.enter_context(nc.sbuf_tensor(name, shape, dt))

        def psum(name, shape):
            return ctx.enter_context(nc.psum_tensor(name, shape, F32))

        def sem(name):
            return ctx.enter_context(nc.semaphore(name))

        slot = psum("slot", [P, 2, 2, 512])
        tp = psum("tp", [P, 2, 512])
        outT = psum("outT", [P, 512])
        back = psum("back", [P, 512])

        ident = sb("ident", [P, P], F32)
        q2 = [sb("q2_hi", [P, HEADS, E], F32R), sb("q2_lo", [P, HEADS, E], F32R)]
        acc = sb("acc", [P, PAIRS, QT, P], F32)
        bk_sb = sb("bk_sb", [P, PAIRS], F32)
        bv_sb = sb("bv_sb", [P, PAIRS], F32)
        b1_sb = sb("b1_sb", [P, FT], F32)
        bo_sb = sb("bo_sb", [P, DM], F32)
        b2_sb = sb("b2_sb", [P, DM], F32)
        negmax_old = sb("negmax_old", [P, PAIRS, U], F32)
        negmax = sb("negmax", [P, PAIRS, U], F32)
        drop = sb("drop", [P, PAIRS, U], F32)
        alpha = sb("alpha", [P, PAIRS, U], F32)
        psumrow = sb("psumrow", [P, PAIRS, U], F32)
        total = sb("total", [P, PAIRS, U], F32)
        inv = sb("inv", [P, PAIRS, U], F32)

        att = ctx.enter_context(ExitStack())
        wk2 = [sb("wk_hi", [P, DC, INNER], F32R, att), sb("wk_lo", [P, DC, INNER], F32R, att)]
        wv2 = [sb("wv_hi", [P, DC, INNER], F32R, att), sb("wv_lo", [P, DC, INNER], F32R, att)]
        x_raw = sb("x_raw", [P, DC, CHUNK], F32, att)
        x2 = [sb("x_hi", [P, DC, CHUNK], F32R, att), sb("x_lo", [P, DC, CHUNK], F32R, att)]
        kst = sb("kst", [P, HEADS, CHUNK], F32R, att)
        val = sb("val", [P, KT, INNER], F32, att)
        mask_raw = sb("mask_raw", [P, QT, CHUNK], U8, att)
        lower = sb("lower", [P, QT, CHUNK], BF16, att)
        pT = sb("pT", [P, 4, E], F32, att)
        outT_sb = sb("outT_sb", [P, E], F32, att)
        pro = att.enter_context(ExitStack())
        prob = sb("prob", [P, 2, U, CHUNK], F32, pro)
        pro.close()
        pre = att.enter_context(ExitStack())
        mt_raw = sb("mt_raw", [P, MC, E], F32, pre)
        wq_raw = sb("wq_raw", [P, MC, INNER], F32, pre)
        mt2 = [sb("mt_hi", [P, MC, E], F32R, pre), sb("mt_lo", [P, MC, E], F32R, pre)]
        wq2 = [sb("wq_hi", [P, MC, INNER], F32R, pre), sb("wq_lo", [P, MC, INNER], F32R, pre)]
        wk_raw = sb("wk_raw", [P, DC, INNER], F32, pre)
        wv_raw = sb("wv_raw", [P, DC, INNER], F32, pre)
        pre.close()
        att.close()

        ao2 = [sb("ao_hi", [P, PAIRS, E], F32R), sb("ao_lo", [P, PAIRS, E], F32R)]
        wo_raw = sb("wo_raw", [P, PAIRS, DM], F32)
        wo2 = [sb("wo_hi", [P, PAIRS, DM], F32R), sb("wo_lo", [P, PAIRS, DM], F32R)]
        m_res = sb("m_res", [P, QT, DM], F32)
        norm = sb("norm", [P, QT, DM], F32)
        stats = sb("stats", [P, QT, 6], F32)
        meanvar = sb("meanvar", [P, QT, 2], F32)
        var_eps = sb("var_eps", [P, QT], F32)
        minus_half = sb("minus_half", [P, 1], F32)
        rstd = sb("rstd", [P, QT], F32)
        mT2 = [sb("mT_hi", [P, MC, E], F32R), sb("mT_lo", [P, MC, E], F32R)]
        w1_raw = sb("w1_raw", [P, 2, MC, P], F32)
        w12 = [sb("w1_hi", [P, 2, MC, P], F32R), sb("w1_lo", [P, 2, MC, P], F32R)]
        w2_raw = sb("w2_raw", [P, 2, DM], F32)
        w22 = [sb("w2_hi", [P, 2, DM], F32R), sb("w2_lo", [P, 2, DM], F32R)]
        hid = sb("hid", [P, 2, E], F32)
        hid2 = [sb("hid_hi", [P, 2, E], F32R), sb("hid_lo", [P, 2, E], F32R)]

        mt_in, wq_in, wk_in, wv_in = sem("mt_in"), sem("wq_in"), sem("wk_in"), sem("wv_in")
        x_in, mask_in, bias_in = sem("x_in"), sem("mask_in"), sem("bias_in")
        wo_in, mres_in = sem("wo_in"), sem("mres_in")
        w1_in, w2_in = [sem("w1_in0"), sem("w1_in1")], [sem("w2_in0"), sem("w2_in1")]
        out_done = sem("out_done")
        zeroed, ident_ready = sem("zeroed"), sem("ident_ready")
        mt_hi, wq_hi, wk_hi, wv_hi = sem("mt_hi_s"), sem("wq_hi_s"), sem("wk_hi_s"), sem("wv_hi_s")
        mt_lo, wq_lo, wk_lo, wv_lo = sem("mt_lo_s"), sem("wq_lo_s"), sem("wk_lo_s"), sem("wv_lo_s")
        xhi_ready, xlo_ready = sem("xhi_ready"), sem("xlo_ready")
        filled = [sem("filled0"), sem("filled1")]
        drained = [sem("drained0"), sem("drained1")]
        qhi_done, khi_done = sem("qhi_done"), sem("khi_done")
        lower_ready = sem("lower_ready")
        exp_done = sem("exp_done")
        tp_filled = [sem("tp_filled0"), sem("tp_filled1")]
        tp_copied = [sem("tp_copied0"), sem("tp_copied1")]
        pv_done = sem("pv_done")
        outT_copied, back_filled = sem("outT_copied"), sem("back_filled")
        acc_scaled, acc_added = sem("acc_scaled"), sem("acc_added")
        drop_ready, alpha_ready = sem("drop_ready"), sem("alpha_ready")
        total_scaled, stats_kept = sem("total_scaled"), sem("stats_kept")
        inv_ready, norm_ready = sem("inv_ready"), sem("norm_ready")
        aoT_filled, aohi, aolo = sem("aoT_filled"), sem("aohi_s"), sem("aolo_s")
        wohi, wolo, mres_ready = sem("wohi_s"), sem("wolo_s"), sem("mres_ready")
        proj_done, m_ready, ln_step, mres2 = sem("proj_done"), sem("m_ready"), sem("ln_step"), sem("mres2")
        mT_filled, mThi, mTlo = sem("mT_filled"), sem("mThi_s"), sem("mTlo_s")
        w1hi, w1lo, w2hi, w2lo = sem("w1hi_s"), sem("w1lo_s"), sem("w2hi_s"), sem("w2lo_s")
        hid_filled, hidhi, hid_f32, hidlo = sem("hid_filled"), sem("hidhi_s"), sem("hid_f32"), sem("hidlo_s")
        half_ready, var_kept = sem("half_ready"), sem("var_kept")
        var_ready, rstd_ready = sem("var_ready"), sem("rstd_ready")
        down_done, z_ready = sem("down_done"), sem("z_ready")

        def in_register(eng, value):
            return value if isinstance(value, int) else eng.to_reg(value)

        def rows(half):
            return slice(DH * half, DH * half + DH)

        def slot_use(c, i):
            g = PRE + i
            return g % 2, c * (BODY // 2) + g // 2

        def slot_plan(sched):
            plan, i = {}, 0
            for step in sched:
                if step[0] in "SVK":
                    plan[step] = i
                    i += 1
            return plan

        def pair_no(c, p):
            return c * PAIRS + p

        def chunks(eng, body):
            body(0, chunk_schedule(True, False))
            mid = chunk_schedule(False, False)
            with eng.Fori(1, CHUNKS - 1) as c:
                body(c, mid)
            body(CHUNKS - 1, chunk_schedule(False, True))

        def hidden_tiles(eng, body):
            for j in range(2):
                body(0, j)
            with eng.Fori(2, FT - 3, 2) as i:
                for j in range(2):
                    body(i, j)
            for j in range(2):
                body(FT - 2, j)

        def per_head(stat, p):
            v = stat[:, p, :].rearrange("p (h t) -> p t h", h=2)
            return v.unsqueeze(3).to_broadcast([P, QT, 2, DH])

        def by_head(t):
            return t.rearrange("p t (h d) -> p t h d", h=2)

        block = ctx.enter_context(nc.Block())

        @block.sync
        def _(sp):
            sp.dma_start(mt_raw[:], mt).then_inc(mt_in, 16)
            sp.dma_start(wq_raw[:], wq).then_inc(wq_in, 16)
            sp.dma_start(wk_raw[:], wk).then_inc(wk_in, 16)
            sp.dma_start(x_raw[:], x[0]).then_inc(x_in, 16)
            sp.dma_start(mask_raw[:], mask[0]).then_inc(mask_in, 16)
            sp.dma_start(bk_sb[:], bk).then_inc(bias_in, 16)
            sp.dma_start(wv_raw[:], wv).then_inc(wv_in, 16)
            sp.dma_start(bv_sb[:], bv).then_inc(bias_in, 16)
            sp.dma_start(b1_sb[:], b1).then_inc(bias_in, 16)
            sp.dma_start(bo_sb[:], bo.to_broadcast([P, DM])).then_inc(bias_in, 16)
            sp.dma_start(b2_sb[:], b2.to_broadcast([P, DM])).then_inc(bias_in, 16)
            with sp.Fori(1, CHUNKS) as c:
                sp.wait_ge(mt_in, 16)
                sp.wait_ge(xhi_ready, c)
                sp.wait_ge(xlo_ready, c)
                sp.wait_ge(lower_ready, c * QT)
                sp.dma_start(x_raw[:], x[bass.ds(c, 1)].rearrange("a p k n -> (a p) k n")).then_inc(x_in, 16)
                sp.dma_start(mask_raw[:], mask[bass.ds(c, 1)].rearrange("a p k n -> (a p) k n")).then_inc(mask_in, 16)
            sp.wait_ge(stats_kept, 2 * CHUNKS * PAIRS)
            sp.wait_ge(acc_added, CHUNKS * PAIRS)
            sp.dma_start(wo_raw[:], wo).then_inc(wo_in, 16)
            sp.dma_start(m_res[:], mn).then_inc(mres_in, 16)
            for j in range(2):
                sp.dma_start(w1_raw[:, j], w1[j]).then_inc(w1_in[j], 16)
                sp.dma_start(w2_raw[:, j], w2[j]).then_inc(w2_in[j], 16)
            with sp.Fori(2, FT - 1, 2) as i:
                for j in range(2):
                    for taken in (w1hi, w1lo, w2hi, w2lo):
                        sp.wait_ge(taken, i - 1 + j)
                    sp.dma_start(w1_raw[:, j], w1[bass.ds(i + j, 1)].rearrange("a p k n -> (a p) k n")).then_inc(w1_in[j], 16)
                    sp.dma_start(w2_raw[:, j], w2[bass.ds(i + j, 1)].rearrange("a p n -> (a p) n")).then_inc(w2_in[j], 16)
            for t in range(QT):
                sp.wait_ge(z_ready, t + 1)
                sp.dma_start(out[t], norm[:, t]).then_inc(out_done, 16)
            sp.wait_ge(out_done, 16 * QT)

        @block.gpsimd
        def _(pool):
            nc.gpsimd.memset(ident[:], 0.0).then_inc(zeroed, 1)
            nc.gpsimd.memset(total[:], 0.0)
            nc.gpsimd.memset(acc[:], 0.0)
            nc.gpsimd.memset(negmax_old[:], 3e38).then_inc(zeroed, 1)
            pool.wait_ge(zeroed, 2)
            nc.gpsimd.affine_select(out=ident[:], in_=ident[:], compare_op=ALU.not_equal, fill=1.0, base=0,
                                    pattern=[[-1, P]], channel_multiplier=1).then_inc(ident_ready, 1)

            def lower_tile(t):
                nc.gpsimd.tensor_scalar(lower[:, t], mask_raw[:, t], -1.0, -BIG, ALU.add, ALU.mult).then_inc(lower_ready, 1)

            pool.wait_ge(x_in, 16)
            pool.wait_ge(xhi_ready, 1)
            nc.gpsimd.tensor_tensor(x2[1][:], x_raw[:], x2[0][:], ALU.subtract).then_inc(xlo_ready, 1)
            pool.wait_ge(mask_in, 16)
            for t in range(QT):
                lower_tile(t)
            pool.wait_ge(wv_hi, 1)
            nc.gpsimd.tensor_tensor(wv2[1][:], wv_raw[:], wv2[0][:], ALU.subtract).then_inc(wv_lo, 1)

            def body(c, sched):
                plan = slot_plan(sched)
                if isinstance(c, int) and c == CHUNKS - 1:
                    pool.wait_ge(lower_ready, CHUNKS * QT)
                    nc.gpsimd.memset(lower[:, :, N - c * CHUNK:], 2 * BIG).then_inc(lower_ready, 1)
                for step in sched:
                    kind, p, i = step
                    if kind == "Z":
                        n = pair_no(c, p)
                        pool.wait_ge(exp_done, n * U + U)
                        nc.gpsimd.tensor_tensor(drop[:, p], negmax[:, p], negmax_old[:, p], ALU.subtract).then_inc(drop_ready, 1)
                        read = in_register(pool, n + 1)
                        pool.wait_ge(zeroed, 2)
                        pool.wait_ge(drop_ready, read)
                        nc.gpsimd.tensor_copy(negmax_old[:, p], negmax[:, p]).then_inc(stats_kept, 1)
                        pool.wait_ge(alpha_ready, n + 1)
                        nc.gpsimd.tensor_tensor(total[:, p], total[:, p], alpha[:, p], ALU.mult).then_inc(total_scaled, 1)
                        pool.wait_ge(total_scaled, n + 1)
                        nc.gpsimd.tensor_tensor(total[:, p], total[:, p], psumrow[:, p], ALU.add).then_inc(stats_kept, 1)
                        if not isinstance(c, int) or c > 0:
                            pool.wait_ge(acc_added, n - PAIRS + 1)
                        nc.gpsimd.tensor_tensor(by_head(acc[:, p]), by_head(acc[:, p]), per_head(alpha, p), ALU.mult).then_inc(acc_scaled, 1)
                    if kind == "X":
                        j, before = slot_use(c, plan[("V", 0, V_SLOTS - 1)])
                        pool.wait_ge(filled[j], before + 1)
                        pool.wait_ge(xhi_ready, c + 2)
                        nc.gpsimd.tensor_tensor(x2[1][:], x_raw[:], x2[0][:], ALU.subtract).then_inc(xlo_ready, 1)
                    if kind == "K" and p == 0:
                        pool.wait_ge(mask_in, 16 * (c + 2))
                        for t in range(QT):
                            j, before = slot_use(c, plan[("S", PAIRS - 1, QT + t)])
                            read = in_register(pool, before + 1)
                            pool.wait_ge(zeroed, 2)
                            pool.wait_ge(drained[j], read)
                            lower_tile(t)

            chunks(pool, body)

            pool.wait_ge(wohi, 1)
            nc.gpsimd.tensor_tensor(wo2[1][:], wo_raw[:], wo2[0][:], ALU.subtract).then_inc(wolo, 1)
            pool.wait_ge(mres_in, 16)
            pool.wait_ge(bias_in, 16 * 5)
            nc.gpsimd.tensor_tensor(m_res[:], m_res[:], bo_sb[:].unsqueeze(1).to_broadcast([P, QT, DM]), ALU.add).then_inc(mres_ready, 1)
            def hidden_lo(i, j):
                pool.wait_ge(hidhi, i + j + 1)
                nc.gpsimd.tensor_tensor(hid2[1][:, j], hid[:, j], hid2[0][:, j], ALU.subtract).then_inc(hidlo, 1)

            def inv_deviation(t, before):
                pool.wait_ge(var_ready, before + t + 1)
                nc.gpsimd.tensor_scalar(var_eps[:, t:t + 1], meanvar[:, t, 1:2], EPS, None, ALU.add).then_inc(var_kept, 1)
                pool.wait_ge(var_kept, before + t + 1)
                nc.gpsimd.tensor_tensor(rstd[:, t:t + 1], var_eps[:, t:t + 1], minus_half[:], ALU.pow).then_inc(rstd_ready, 1)

            nc.gpsimd.memset(minus_half[:], -0.5).then_inc(half_ready, 1)
            pool.wait_ge(half_ready, 1)
            for t in range(QT):
                inv_deviation(t, 0)
            for t in range(QT):
                pool.wait_ge(m_ready, t + 1)
                nc.gpsimd.tensor_tensor(m_res[:, t], norm[:, t], b2_sb[:], ALU.add).then_inc(mres2, 1)
            hidden_tiles(pool, hidden_lo)
            for t in range(QT):
                inv_deviation(t, QT)

        @block.scalar
        def _(act):
            act.wait_ge(mt_in, 16)
            nc.scalar.copy(mt2[0][:], mt_raw[:]).then_inc(mt_hi, 1)
            act.wait_ge(wq_in, 16)
            nc.scalar.copy(wq2[0][:], wq_raw[:]).then_inc(wq_hi, 1)
            act.wait_ge(x_in, 16)
            nc.scalar.copy(x2[0][:], x_raw[:]).then_inc(xhi_ready, 1)
            act.wait_ge(wk_in, 16)
            nc.scalar.copy(wk2[0][:], wk_raw[:]).then_inc(wk_hi, 1)
            act.wait_ge(wv_in, 16)
            nc.scalar.copy(wv2[0][:], wv_raw[:]).then_inc(wv_hi, 1)
            for p in range(PAIRS):
                act.wait_ge(filled[p % 2], p // 2 + 1)
                for half, to in HALVES:
                    last = nc.scalar.activation(q2[0][rows(to), 2 * p + half], slot[rows(half), p % 2, 0], ACT.Identity, scale=-SCALE)
                last.then_inc(qhi_done, 1)

            act.wait_ge(bias_in, 16 * 5)

            def keys_hi(p, j):
                for half in range(2):
                    last = nc.scalar.activation(kst[rows(half), 2 * p + half].rearrange("p (b n) -> p b n", b=2),
                                                slot[rows(half), j, :, :HALF], ACT.Identity, bias=bk_sb[rows(half), p:p + 1])
                last.then_inc(khi_done, 1)

            for p in range(PAIRS):
                g = Q_SLOTS + p
                act.wait_ge(filled[g % 2], g // 2 + 1)
                keys_hi(p, g % 2)

            def body(c, sched):
                plan = slot_plan(sched)
                for step in sched:
                    kind, p, i = step
                    if kind == "E":
                        j, before = slot_use(c, plan[("S", p, i)])
                        act.wait_ge(drained[j], before + 1)
                        unit = prob[:, p % 2, i]
                        nc.scalar.activation(unit, unit, ACT.Exp, bias=negmax[:, p, i:i + 1], scale=-1.0,
                                             accum_out=psumrow[:, p, i:i + 1]).then_inc(exp_done, 1)
                    if kind == "V":
                        j, before = slot_use(c, plan[step])
                        n = min(2, KT - 2 * i)
                        act.wait_ge(filled[j], before + 1)
                        nc.scalar.copy(val[:, 2 * i:2 * i + n], slot[:, j, :n]).then_inc(drained[j], 1)
                    if kind == "K":
                        j, before = slot_use(c, plan[step])
                        act.wait_ge(filled[j], before + 1)
                        keys_hi(p, j)
                    if kind == "T" and i % 2 == 0:
                        n = pair_no(c, p) * TV + i
                        act.wait_ge(tp_filled[0], pair_no(c, p) * KT + i // 2 + 1)
                        if not isinstance(n, int) or n >= 4:
                            act.wait_ge(pv_done, n - 3)
                        nc.scalar.copy(pT[:, (p * TV + i) % 4], tp[:, 0]).then_inc(tp_copied[0], 1)
                    if kind == "C":
                        n = pair_no(c, p)
                        act.wait_ge(pv_done, (n + 1) * TV)
                        if not isinstance(n, int) or n >= 1:
                            act.wait_ge(back_filled, n)
                        nc.scalar.copy(outT_sb[:], outT[:]).then_inc(outT_copied, 1)
                    if kind == "Z":
                        act.wait_ge(drop_ready, pair_no(c, p) + 1)
                        nc.scalar.activation(alpha[:, p], drop[:, p], ACT.Exp).then_inc(alpha_ready, 1)
                    if kind == "X":
                        j, before = slot_use(c, plan[("V", 0, V_SLOTS - 1)])
                        act.wait_ge(filled[j], before + 1)
                        act.wait_ge(x_in, 16 * (c + 2))
                        nc.scalar.copy(x2[0][:], x_raw[:]).then_inc(xhi_ready, 1)

            chunks(act, body)

            act.wait_ge(wo_in, 16)
            nc.scalar.copy(wo2[0][:], wo_raw[:]).then_inc(wohi, 1)

            def up_weights_hi(n, j):
                act.wait_ge(w1_in[j], (n - j) * 8 + 16)
                nc.scalar.copy(w12[0][:, j], w1_raw[:, j]).then_inc(w1hi, 1)

            def down_weights_hi(n, j):
                act.wait_ge(w2_in[j], (n - j) * 8 + 16)
                nc.scalar.copy(w22[0][:, j], w2_raw[:, j]).then_inc(w2hi, 1)

            for p in range(PAIRS):
                act.wait_ge(aoT_filled, p + 1)
                nc.scalar.activation(ao2[0][:, p], tp[:, p % 2], ACT.Identity, bias=bv_sb[:, p:p + 1]).then_inc(aohi, 1)
            up_weights_hi(0, 0)
            up_weights_hi(1, 1)
            down_weights_hi(0, 0)
            for k in range(MC):
                act.wait_ge(mT_filled, k + 1)
                nc.scalar.copy(mT2[0][:, k], tp[:, k % 2]).then_inc(mThi, 1)

            def hidden_f32(i, j):
                n = i + j
                act.wait_ge(hid_filled, n + 1)
                if not isinstance(n, int) or n >= 2:
                    act.wait_ge(hidlo, n - 1)
                nc.scalar.activation(hid[:, j], tp[:, j], ACT.Relu, bias=b1_sb[:, bass.ds(n, 1)]).then_inc(hid_f32, 1)
                if not isinstance(n, int) or n + 2 < FT:
                    up_weights_hi(n + 2, j)
                if not isinstance(n, int) or n + 1 < FT:
                    if not isinstance(n, int) or n > 0:
                        act.wait_ge(down_done, n)
                    down_weights_hi(n + 1, 1 - j)

            hidden_tiles(act, hidden_f32)

        @block.vector
        def _(dve):
            dve.wait_ge(mt_hi, 1)
            nc.vector.tensor_tensor(mt2[1][:], mt_raw[:], mt2[0][:], ALU.subtract).then_inc(mt_lo, 1)
            dve.wait_ge(wq_hi, 1)
            nc.vector.tensor_tensor(wq2[1][:], wq_raw[:], wq2[0][:], ALU.subtract).then_inc(wq_lo, 1)
            dve.wait_ge(wk_hi, 1)
            nc.vector.tensor_tensor(wk2[1][:], wk_raw[:], wk2[0][:], ALU.subtract).then_inc(wk_lo, 1)
            for p in range(PAIRS):
                dve.wait_ge(qhi_done, p + 1)
                for half, to in HALVES:
                    last = nc.vector.scalar_tensor_tensor(out=q2[1][rows(to), 2 * p + half], in0=slot[rows(half), p % 2, 0],
                                                          scalar=-SCALE, in1=q2[0][rows(half), 2 * p + half],
                                                          op0=ALU.mult, op1=ALU.subtract)
                last.then_inc(drained[p % 2], 1)

            dve.wait_ge(bias_in, 16 * 5)

            def keys_lo(p, j, before):
                for half in range(2):
                    last = nc.vector.scalar_tensor_tensor(
                        out=kst[rows(1 - half), 2 * p + half].rearrange("p (b n) -> p b n", b=2),
                        in0=slot[rows(half), j, :, :HALF], scalar=bk_sb[rows(half), p:p + 1],
                        in1=kst[rows(half), 2 * p + half].rearrange("p (b n) -> p b n", b=2), op0=ALU.add, op1=ALU.subtract)
                last.then_inc(drained[j], 1)

            for p in range(PAIRS):
                g = Q_SLOTS + p
                dve.wait_ge(khi_done, p + 1)
                keys_lo(p, g % 2, 0)

            dve.wait_ge(zeroed, 2)
            def body(c, sched):
                plan = slot_plan(sched)
                for step in sched:
                    kind, p, i = step
                    if kind == "S":
                        j, before = slot_use(c, plan[step])
                        t = i % QT
                        final = isinstance(c, int) and c == CHUNKS - 1
                        written = in_register(dve, before + 1)
                        masks = taken = None
                        if p == 0 and (i == 0 if final else i < QT):
                            masks = in_register(dve, CHUNKS * QT + 1 if final else c * QT + t + 1)
                        if i == 0 and (not isinstance(c, int) or c > 0):
                            taken = in_register(dve, 2 * (pair_no(c, p) - PAIRS + 1))
                        dve.wait_ge(zeroed, 2)
                        if masks is not None:
                            dve.wait_ge(lower_ready, masks)
                        if taken is not None:
                            dve.wait_ge(stats_kept, taken)
                        dve.wait_ge(filled[j], written)
                        nc.vector.tensor_tensor_reduce(
                            out=prob[:, p % 2, i].rearrange("p (b n) -> p b n", b=2),
                            in0=slot[:, j, :, :HALF], in1=lower[:, t].rearrange("p (b n) -> p b n", b=2),
                            scale=1.0, scalar=negmax_old[:, p, i:i + 1], op0=ALU.add, op1=ALU.min,
                            accum_out=negmax[:, p, i:i + 1]).then_inc(drained[j], 1)
                    if kind == "K":
                        j, before = slot_use(c, plan[step])
                        dve.wait_ge(khi_done, (c + 1) * PAIRS + p + 1)
                        keys_lo(p, j, before)
                    if kind == "T" and i % 2 == 1:
                        n = pair_no(c, p) * TV + i
                        dve.wait_ge(tp_filled[1], pair_no(c, p) * KT + i // 2 + 1)
                        if not isinstance(n, int) or n >= 4:
                            dve.wait_ge(pv_done, n - 3)
                        nc.vector.tensor_copy(pT[:, (p * TV + i) % 4], tp[:, 1]).then_inc(tp_copied[1], 1)
                    if kind == "A":
                        n = pair_no(c, p)
                        dve.wait_ge(acc_scaled, n + 1)
                        dve.wait_ge(back_filled, n + 1)
                        own = acc[:, p % PAIRS].rearrange("p t n -> p (t n)")
                        nc.vector.tensor_tensor(own, own, back[:], ALU.add).then_inc(acc_added, 1)

            chunks(dve, body)

            dve.wait_ge(stats_kept, 2 * CHUNKS * PAIRS)
            dve.wait_ge(acc_added, CHUNKS * PAIRS)
            nc.vector.reciprocal(inv[:], total[:]).then_inc(inv_ready, 1)
            dve.wait_ge(inv_ready, 1)
            for p in range(PAIRS):
                nc.vector.tensor_tensor(by_head(acc[:, p]), by_head(acc[:, p]), per_head(inv, p), ALU.mult).then_inc(norm_ready, 1)
            for p in range(PAIRS):
                dve.wait_ge(aohi, p + 1)
                nc.vector.scalar_tensor_tensor(out=ao2[1][:, p], in0=tp[:, p % 2], scalar=bv_sb[:, p:p + 1], in1=ao2[0][:, p],
                                               op0=ALU.add, op1=ALU.subtract).then_inc(aolo, 1)

            def layer_norm(t, src, count):
                nc.vector.tensor_tensor(norm[:, t], src, m_res[:, t], ALU.add).then_inc(ln_step, 1)
                dve.wait_ge(ln_step, count + 1)
                nc.vector.bn_stats(stats[:, t], norm[:, t]).then_inc(ln_step, 1)
                dve.wait_ge(ln_step, count + 2)
                nc.vector.bn_aggr(meanvar[:, t], stats[:, t]).then_inc(var_ready, 1)

            def layer_scale(t, before, done):
                dve.wait_ge(rstd_ready, before + t + 1)
                nc.vector.tensor_scalar(norm[:, t], norm[:, t], meanvar[:, t, 0:1], rstd[:, t:t + 1],
                                        ALU.subtract, ALU.mult).then_inc(done, 1)

            def up_weights_lo(n, j):
                dve.wait_ge(w1hi, n + 1)
                nc.vector.tensor_tensor(w12[1][:, j], w1_raw[:, j], w12[0][:, j], ALU.subtract).then_inc(w1lo, 1)

            def down_weights_lo(n, j):
                dve.wait_ge(w2hi, n + 1)
                nc.vector.tensor_tensor(w22[1][:, j], w2_raw[:, j], w22[0][:, j], ALU.subtract).then_inc(w2lo, 1)

            dve.wait_ge(mres_ready, 1)
            for t in range(QT):
                dve.wait_ge(proj_done, t + 1)
                layer_norm(t, slot[:, t // 2, t % 2], 2 * t)
                if t >= 1:
                    layer_scale(t - 1, 0, m_ready)
            layer_scale(QT - 1, 0, m_ready)
            up_weights_lo(0, 0)
            up_weights_lo(1, 1)
            down_weights_lo(0, 0)
            for k in range(MC):
                dve.wait_ge(mThi, k + 1)
                nc.vector.tensor_tensor(mT2[1][:, k], tp[:, k % 2], mT2[0][:, k], ALU.subtract).then_inc(mTlo, 1)

            def hidden_hi(i, j):
                n = i + j
                dve.wait_ge(hid_f32, n + 1)
                nc.vector.tensor_copy(hid2[0][:, j], hid[:, j]).then_inc(hidhi, 1)
                if not isinstance(n, int) or n + 2 < FT:
                    up_weights_lo(n + 2, j)
                if not isinstance(n, int) or n + 1 < FT:
                    down_weights_lo(n + 1, 1 - j)

            hidden_tiles(dve, hidden_hi)
            dve.wait_ge(mres2, QT)
            for t in range(QT):
                dve.wait_ge(down_done, FT)
                layer_norm(t, slot[:, t // 2, t % 2], 2 * (QT + t))
                if t >= 1:
                    layer_scale(t - 1, QT, z_ready)
            layer_scale(QT - 1, QT, z_ready)

        @block.tensor
        def _(pe):
            def products(dst, stationary, moving, terms):
                for n, (a, b, k) in enumerate(terms):
                    last = nc.tensor.matmul(dst, stationary(a, k), moving(b, k), start=(n == 0), stop=(n == len(terms) - 1))
                return last

            def split(width):
                return [(a, b, k) for a, b in TERMS for k in range(width)]

            pe.wait_ge(mt_hi, 1)
            pe.wait_ge(wq_hi, 1)
            pe.wait_ge(mt_lo, 1)
            pe.wait_ge(wq_lo, 1)
            for p in range(PAIRS):
                if p >= 2:
                    pe.wait_ge(drained[p % 2], p // 2)
                products(slot[:, p % 2, 0], lambda a, k: wq2[a][:, k, P * p:P * p + P],
                         lambda b, k: mt2[b][:, k], split(MC)).then_inc(filled[p % 2], 1)

            def keys(p, j):
                for b in range(2):
                    last = products(slot[:, j, b, :HALF], lambda a, k: wk2[a][:, k, P * p:P * p + P],
                                    lambda m, k: x2[m][:, k, b * HALF:b * HALF + HALF], split(DC))
                return last

            pe.wait_ge(wk_hi, 1)
            pe.wait_ge(wk_lo, 1)
            pe.wait_ge(xhi_ready, 1)
            pe.wait_ge(xlo_ready, 1)
            for p in range(PAIRS):
                g = Q_SLOTS + p
                pe.wait_ge(drained[g % 2], g // 2)
                keys(p, g % 2).then_inc(filled[g % 2], 1)

            pe.wait_ge(wv_hi, 1)
            pe.wait_ge(wv_lo, 1)
            pe.wait_ge(ident_ready, 1)

            def body(c, sched):
                plan = slot_plan(sched)
                for step in sched:
                    kind, p, i = step
                    if step in plan:
                        j, before = slot_use(c, plan[step])
                        pe.wait_ge(drained[j], before)
                    if kind == "S":
                        h, t = 2 * p + i // QT, i % QT
                        for part in range(2):
                            for b in range(2):
                                last = nc.tensor.matmul(slot[:, j, b, :HALF], q2[part][:, h, P * t:P * t + P],
                                                        kst[:, h, b * HALF:b * HALF + HALF], start=(part == 0), stop=(part == 1))
                        last.then_inc(filled[j], 1)
                    if kind == "V":
                        for n in range(min(2, KT - 2 * i)):
                            kt = 2 * i + n
                            last = products(slot[:, j, n], lambda a, k: x2[a][:, k, P * kt:P * kt + P],
                                            lambda m, k: wv2[m][:, k], split(DC))
                        last.then_inc(filled[j], 1)
                    if kind == "K":
                        if p == 0:
                            pe.wait_ge(xhi_ready, c + 2)
                            pe.wait_ge(xlo_ready, c + 2)
                        keys(p, j).then_inc(filled[j], 1)
                    if kind == "T":
                        h, kt = i // KT, i % KT
                        if kt == 0:
                            pe.wait_ge(exp_done, pair_no(c, p) * U + QT * (h + 1))
                        if not isinstance(c, int) or pair_no(c, p) > 0 or i >= 2:
                            pe.wait_ge(tp_copied[i % 2], pair_no(c, p) * KT + i // 2)
                        for t in range(QT):
                            last = nc.tensor.transpose(tp[:, i % 2, P * t:P * t + P],
                                                       prob[:, p % 2, h * QT + t, P * kt:P * kt + P], ident[:])
                        last.then_inc(tp_filled[i % 2], 1)
                    if kind == "W":
                        h, kt = i // KT, i % KT
                        if i == 0:
                            if p == 0:
                                for v in (V_SLOTS - 2, V_SLOTS - 1):
                                    vj, v_before = slot_use(c, plan[("V", 0, v)])
                                    pe.wait_ge(drained[vj], v_before + 1)
                            if not isinstance(c, int) or pair_no(c, p) > 0:
                                pe.wait_ge(outT_copied, pair_no(c, p))
                        pe.wait_ge(tp_copied[i % 2], pair_no(c, p) * KT + i // 2 + 1)
                        nc.tensor.matmul(outT[DH * h:DH * h + DH], val[:, kt, P * p + DH * h:P * p + DH * h + DH],
                                         pT[:, (p * TV + i) % 4], start=(kt == 0), stop=(kt == KT - 1)).then_inc(pv_done, 1)
                    if kind == "F":
                        n = pair_no(c, p)
                        pe.wait_ge(outT_copied, n + 1)
                        if not isinstance(n, int) or n >= 1:
                            pe.wait_ge(acc_added, n)
                        for t in range(QT):
                            last = nc.tensor.transpose(back[:, P * t:P * t + P], outT_sb[:, P * t:P * t + P], ident[:])
                        last.then_inc(back_filled, 1)

            chunks(pe, body)

            for p in range(PAIRS):
                pe.wait_ge(norm_ready, p + 1)
                if p >= 2:
                    pe.wait_ge(aolo, p - 1)
                for t in range(QT):
                    last = nc.tensor.transpose(tp[:, p % 2, P * t:P * t + P], acc[:, p, t], ident[:])
                last.then_inc(aoT_filled, 1)
            pe.wait_ge(wohi, 1)
            pe.wait_ge(wolo, 1)
            pe.wait_ge(aolo, PAIRS)
            for t in range(QT):
                products(slot[:, t // 2, t % 2], lambda a, k: ao2[a][:, k, P * t:P * t + P],
                         lambda b, k: wo2[b][:, k], split(PAIRS)).then_inc(proj_done, 1)
            pe.wait_ge(m_ready, QT)
            for k in range(MC):
                if k >= 2:
                    pe.wait_ge(mTlo, k - 1)
                for t in range(QT):
                    last = nc.tensor.transpose(tp[:, k % 2, P * t:P * t + P], norm[:, t, P * k:P * k + P], ident[:])
                last.then_inc(mT_filled, 1)

            def up(n, j):
                pe.wait_ge(w1lo, n + 1)
                if not isinstance(n, int) or n >= 2:
                    pe.wait_ge(hid_f32, n - 1)
                products(tp[:, j], lambda a, k: w12[a][:, j, k], lambda b, k: mT2[b][:, k], split(MC)).then_inc(hid_filled, 1)

            def down(n, j, first, last_one):
                pe.wait_ge(w2lo, n + 1)
                pe.wait_ge(hidlo, n + 1)
                for t in range(QT):
                    for i, (a, b) in enumerate(TERMS):
                        last = nc.tensor.matmul(slot[:, t // 2, t % 2], hid2[a][:, j, P * t:P * t + P], w22[b][:, j],
                                                start=first and i == 0, stop=last_one and i == len(TERMS) - 1)
                last.then_inc(down_done, 1)

            pe.wait_ge(mTlo, MC)
            up(0, 0)
            up(1, 1)
            down(0, 0, True, False)
            with pe.Fori(2, FT - 1, 2) as i:
                up(i, 0)
                down(i - 1, 1, False, False)
                up(i + 1, 1)
                down(i, 0, False, False)
            down(FT - 1, 1, False, True)


def layouts(a):
    import numpy as np

    x = np.zeros((NPAD, D), np.float32)
    x[:N] = a["L0_rec_x"]
    mask = np.zeros((E, NPAD), bool)
    mask[:, :N] = a["r_mask"].reshape(E, N)
    m = a["r_M"]
    wkv = a["L0_rec_Wkv"]
    bkv = a["L0_rec_bkv"]

    def rows(w, k):
        return w.T.reshape(k, P, -1).transpose(1, 0, 2)

    return {
        "x": x.reshape(CHUNKS, CHUNK, DC, P).transpose(0, 3, 2, 1),
        "mask": mask.reshape(QT, P, CHUNKS, CHUNK).transpose(2, 1, 0, 3),
        "mt": rows(m, MC),
        "mn": m.reshape(QT, P, DM).transpose(1, 0, 2),
        "wq": rows(a["L0_rec_Wq"], MC),
        "wk": rows(wkv[:INNER], DC),
        "wv": rows(wkv[INNER:], DC),
        "bk": bkv[:INNER].reshape(PAIRS, P).T,
        "bv": bkv[INNER:].reshape(PAIRS, P).T,
        "wo": rows(a["L0_rec_Wo"], PAIRS),
        "bo": a["L0_rec_bo"].reshape(1, DM),
        "w1": a["L0_rec_W1"].reshape(FT, P, MC, P).transpose(0, 3, 2, 1),
        "b1": a["L0_rec_b1"].reshape(FT, P).T,
        "w2": a["L0_rec_W2"].T.reshape(FT, P, DM),
        "b2": a["L0_rec_b2"].reshape(1, DM),
    }


def kernel(**inputs):
    import numpy as np
    import concourse.bacc as bacc
    from concourse.bass_utils import run_bass_kernel_spmd

    arrays = {f"in_{k}": np.ascontiguousarray(v) for k, v in layouts({k: np.asarray(v) for k, v in inputs.items()}).items()}
    nc = bacc.Bacc("TRN2", target_bir_lowering=False, num_devices=1)
    aps = {k[3:]: nc.dram_tensor(k, v.shape, mybir.dt.from_np(v.dtype), kind="ExternalInput").ap() for k, v in arrays.items()}
    out = nc.dram_tensor("out_z", (QT, P, DM), F32, kind="ExternalOutput").ap()
    build(nc, **aps, out=out)
    r = run_bass_kernel_spmd(nc, [arrays], core_ids=[0])
    return r.results[0]["out_z"].reshape(E, DM)
```

```python
from contextlib import ExitStack

import concourse.bass as bass
from concourse import mybir
from concourse.alu_op_type import AluOpType as ALU

ACT = mybir.ActivationFunctionType
F32 = mybir.dt.float32
F32R = mybir.dt.float32r
BF16 = mybir.dt.bfloat16
U8 = mybir.dt.uint8

P = 128
E = 512
N = 6250
D = 256
DM = 512
INNER = 512
HEADS = 8
DH = 64
FF = 2048
QT = E // P
PAIRS = HEADS // 2
U = 2 * QT
KT = 7
CHUNK = KT * P
CHUNKS = -(-N // CHUNK)
NPAD = CHUNKS * CHUNK
HALF = CHUNK // 2
TV = 2 * KT
FT = FF // P
DC = D // P
MC = DM // P
KEYS_AT = 3
BIG = 2.0 ** 100
EPS = 1e-5
HALVES = [(half, to) for half in range(2) for to in range(2)]
SCALE = DH ** -0.5

TERMS = ((0, 0), (0, 1), (1, 0))

Q_SLOTS = PAIRS
V_SLOTS = -(-KT // 2)
PRE = Q_SLOTS + 2
ACT_COPIES = (0, 1, 2, 4, 6, 8, 10, 12)
TP_USES = (TV + 1) // 3
BODY = PAIRS * U + V_SLOTS + PAIRS


def chunk_schedule(first, last):
    out = []

    def products(p, start, keys, ahead):
        done = start
        parts = [[("K", k, 0), ("H", k, 0)] if i == 0 else [("H", k, 1), ("L", k, 0)] if i == 1 else [("L", k, 1)]
                 for k in keys for i in range(3)]
        while ahead < 2:
            out.append(("T", p, ahead))
            ahead += 1
        if p + 1 < PAIRS:
            out.append(("E", p + 1, start - 1))
        for k in range(KT):
            while ahead < min(TV, 2 * k + 4):
                out.append(("T", p, ahead))
                ahead += 1
            out.extend([("W", p, 2 * k), ("W", p, 2 * k + 1)])
            if k == 1:
                out.append(("Z", p, 0))
            if p + 1 < PAIRS and done < U:
                for _ in range(2):
                    if done < U:
                        out.extend([("S", p + 1, done)])
                        if done > start:
                            out.append(("E", p + 1, done - 1))
                        done += 1
                if done == U:
                    out.append(("E", p + 1, U - 1))
            elif k >= KEYS_AT:
                for _ in range(len(keys)):
                    if parts:
                        out.extend(parts.pop(0))
        for part in parts:
            out.extend(part)

    def output(p):
        return [] if first and p < 0 else [("F", p, 0), ("A", p, 0)]

    for p in range(PAIRS):
        keys = (2, 3) if p == 0 else () if p == 1 or last else (PAIRS + p - 2,)
        copy = [] if first and p <= 1 else [("C", p - 2, 0)]
        if p == 1:
            out.extend([("V", 0, 0), *copy, ("S", 1, 0), *output(-1), ("T", 0, 0),
                        ("V", 0, 1), ("S", 1, 1), ("E", 1, 0), ("T", 0, 1),
                        ("V", 0, 2), ("S", 1, 2), ("E", 1, 1), ("T", 0, 2), ("V", 0, 3)])
            if not last:
                out.append(("X", 0, 0))
            products(0, 3, keys, 3)
            continue
        out.extend([("S", p, 0), *copy, *output(p - 2), ("S", p, 1)])
        if first and p == 0:
            for i in range(2, U):
                out.extend([("E", p, i - 2), ("S", p, i)])
            out.extend([("E", p, U - 2), ("E", p, U - 1)])
            for k in keys:
                out.extend([("K", k, 0), ("H", k, 0), ("H", k, 1), ("L", k, 0), ("L", k, 1)])
        else:
            out.extend([("T", p - 1, 0), ("T", p - 1, 1), ("E", p, 0)])
            products(p - 1, 2, keys, 2)
    if last:
        tail = PAIRS - 1
        out.extend([("C", tail - 1, 0), *output(tail - 1)])
        products(tail, U, (), 0)
        out.extend([("C", tail, 0), *output(tail)])
    return out


def build(nc, x, mask, mt, mn, wq, wk, wv, bk, bv, wo, bo, w1, b1, w2, b2, out):
    with ExitStack() as ctx:
        def sb(name, shape, dt, where=ctx):
            return where.enter_context(nc.sbuf_tensor(name, shape, dt))

        def psum(name, shape):
            return ctx.enter_context(nc.psum_tensor(name, shape, F32))

        def sem(name):
            return ctx.enter_context(nc.semaphore(name))

        slot = psum("slot", [P, 2, 2, 512])
        tp = psum("tp", [P, 3, 512])
        outT = psum("outT", [P, 512])

        ident = sb("ident", [P, P], F32)
        q2 = [sb("q2_hi", [P, HEADS, E], F32R), sb("q2_lo", [P, HEADS, E], F32R)]
        acc = sb("acc", [P, PAIRS, QT, P], F32)
        bk_sb = sb("bk_sb", [P, PAIRS], F32)
        bv_sb = sb("bv_sb", [P, PAIRS], F32)
        b1_sb = sb("b1_sb", [P, FT], F32)
        bo_sb = sb("bo_sb", [P, DM], F32)
        b2_sb = sb("b2_sb", [P, DM], F32)
        negmax_old = sb("negmax_old", [P, PAIRS, U], F32)
        negmax = sb("negmax", [P, PAIRS, U], F32)
        drop = sb("drop", [P, PAIRS, U], F32)
        alpha = sb("alpha", [P, PAIRS, U], F32)
        psumrow = sb("psumrow", [P, PAIRS, U], F32)
        total = sb("total", [P, PAIRS, U], F32)
        inv = sb("inv", [P, PAIRS, U], F32)

        att = ctx.enter_context(ExitStack())
        wk2 = [sb("wk_hi", [P, DC, INNER], F32R, att), sb("wk_lo", [P, DC, INNER], F32R, att)]
        wv2 = [sb("wv_hi", [P, DC, INNER], F32R, att), sb("wv_lo", [P, DC, INNER], F32R, att)]
        x_raw = sb("x_raw", [P, DC, CHUNK], F32, att)
        x2 = [sb("x_hi", [P, DC, CHUNK], F32R, att), sb("x_lo", [P, DC, CHUNK], F32R, att)]
        kst = sb("kst", [P, HEADS, CHUNK], F32R, att)
        val = sb("val", [P, KT, INNER], F32, att)
        mask_raw = sb("mask_raw", [P, QT, CHUNK], U8, att)
        lower = sb("lower", [P, QT, CHUNK], BF16, att)
        pT = sb("pT", [P, 4, E], F32, att)
        outT_sb = sb("outT_sb", [P, E], F32, att)
        pro = att.enter_context(ExitStack())
        prob = sb("prob", [P, 2, U, CHUNK], F32, pro)
        pro.close()
        pre = att.enter_context(ExitStack())
        mt_raw = sb("mt_raw", [P, MC, E], F32, pre)
        wq_raw = sb("wq_raw", [P, MC, INNER], F32, pre)
        mt2 = [sb("mt_hi", [P, MC, E], F32R, pre), sb("mt_lo", [P, MC, E], F32R, pre)]
        wq2 = [sb("wq_hi", [P, MC, INNER], F32R, pre), sb("wq_lo", [P, MC, INNER], F32R, pre)]
        wk_raw = sb("wk_raw", [P, DC, INNER], F32, pre)
        wv_raw = sb("wv_raw", [P, DC, INNER], F32, pre)
        pre.close()
        att.close()

        ao2 = [sb("ao_hi", [P, PAIRS, E], F32R), sb("ao_lo", [P, PAIRS, E], F32R)]
        wo_raw = sb("wo_raw", [P, PAIRS, DM], F32)
        wo2 = [sb("wo_hi", [P, PAIRS, DM], F32R), sb("wo_lo", [P, PAIRS, DM], F32R)]
        m_res = sb("m_res", [P, QT, DM], F32)
        norm = sb("norm", [P, QT, DM], F32)
        stats = sb("stats", [P, QT, 6], F32)
        meanvar = sb("meanvar", [P, QT, 2], F32)
        var_eps = sb("var_eps", [P, QT], F32)
        minus_half = sb("minus_half", [P, 1], F32)
        rstd = sb("rstd", [P, QT], F32)
        mT2 = [sb("mT_hi", [P, MC, E], F32R), sb("mT_lo", [P, MC, E], F32R)]
        w1_raw = sb("w1_raw", [P, 2, MC, P], F32)
        w12 = [sb("w1_hi", [P, 2, MC, P], F32R), sb("w1_lo", [P, 2, MC, P], F32R)]
        w2_raw = sb("w2_raw", [P, 2, DM], F32)
        w22 = [sb("w2_hi", [P, 2, DM], F32R), sb("w2_lo", [P, 2, DM], F32R)]
        hid = sb("hid", [P, 2, E], F32)
        hid2 = [sb("hid_hi", [P, 2, E], F32R), sb("hid_lo", [P, 2, E], F32R)]

        mt_in, wq_in, wk_in, wv_in = sem("mt_in"), sem("wq_in"), sem("wk_in"), sem("wv_in")
        x_in, mask_in, bias_in = sem("x_in"), sem("mask_in"), sem("bias_in")
        wo_in, mres_in = sem("wo_in"), sem("mres_in")
        w1_in, w2_in = [sem("w1_in0"), sem("w1_in1")], [sem("w2_in0"), sem("w2_in1")]
        out_done = sem("out_done")
        zeroed, ident_ready = sem("zeroed"), sem("ident_ready")
        mt_hi, wq_hi, wk_hi, wv_hi = sem("mt_hi_s"), sem("wq_hi_s"), sem("wk_hi_s"), sem("wv_hi_s")
        mt_lo, wq_lo, wk_lo, wv_lo = sem("mt_lo_s"), sem("wq_lo_s"), sem("wk_lo_s"), sem("wv_lo_s")
        xhi_ready, xlo_ready = sem("xhi_ready"), sem("xlo_ready")
        filled = [sem("filled0"), sem("filled1")]
        drained = [sem("drained0"), sem("drained1")]
        qhi_done, khi_done = sem("qhi_done"), sem("khi_done")
        lower_ready = sem("lower_ready")
        exp_done = sem("exp_done")
        tp_filled = [sem(f"tp_filled{b}") for b in range(3)]
        tp_copied = [sem(f"tp_copied{b}") for b in range(3)]
        pv_done = sem("pv_done")
        outT_copied = sem("outT_copied")
        acc_scaled = sem("acc_scaled")
        drop_ready, alpha_ready = sem("drop_ready"), sem("alpha_ready")
        total_scaled, stats_kept = sem("total_scaled"), sem("stats_kept")
        inv_ready, norm_ready = sem("inv_ready"), sem("norm_ready")
        aoT_filled, aohi, aolo = sem("aoT_filled"), sem("aohi_s"), sem("aolo_s")
        wohi, wolo, mres_ready = sem("wohi_s"), sem("wolo_s"), sem("mres_ready")
        proj_done, m_ready, ln_step, mres2 = sem("proj_done"), sem("m_ready"), sem("ln_step"), sem("mres2")
        mT_filled, mThi, mTlo = sem("mT_filled"), sem("mThi_s"), sem("mTlo_s")
        w1hi, w1lo, w2hi, w2lo = sem("w1hi_s"), sem("w1lo_s"), sem("w2hi_s"), sem("w2lo_s")
        hid_filled, hidhi, hid_f32, hidlo = sem("hid_filled"), sem("hidhi_s"), sem("hid_f32"), sem("hidlo_s")
        half_ready, var_kept = sem("half_ready"), sem("var_kept")
        var_ready, rstd_ready = sem("var_ready"), sem("rstd_ready")
        down_done, z_ready = sem("down_done"), sem("z_ready")

        def in_register(eng, value):
            return value if isinstance(value, int) else eng.to_reg(value)

        def rows(half):
            return slice(DH * half, DH * half + DH)

        def slot_use(c, i):
            g = PRE + i
            return g % 2, c * (BODY // 2) + g // 2

        def slot_plan(sched):
            plan, i = {}, 0
            for step in sched:
                if step[0] in "SVK":
                    plan[step] = i
                    i += 1
            return plan

        def pair_no(c, p):
            return c * PAIRS + p

        def tp_use(n, i):
            return i % 3, n * TP_USES + i // 3

        def chunks(eng, body):
            body(0, chunk_schedule(True, False))
            mid = chunk_schedule(False, False)
            with eng.Fori(1, CHUNKS - 1) as c:
                body(c, mid)
            body(CHUNKS - 1, chunk_schedule(False, True))

        def hidden_tiles(eng, body):
            for j in range(2):
                body(0, j)
            with eng.Fori(2, FT - 3, 2) as i:
                for j in range(2):
                    body(i, j)
            for j in range(2):
                body(FT - 2, j)

        def per_head(stat, p):
            v = stat[:, p, :].rearrange("p (h t) -> p t h", h=2)
            return v.unsqueeze(3).to_broadcast([P, QT, 2, DH])

        def head(p, h):
            start = P * (p % PAIRS) + DH * h
            return slice(start, start + DH)

        def by_head(t):
            return t.rearrange("p t (h d) -> p t h d", h=2)

        block = ctx.enter_context(nc.Block())

        @block.sync
        def _(sp):
            sp.dma_start(mt_raw[:], mt).then_inc(mt_in, 16)
            sp.dma_start(wq_raw[:], wq).then_inc(wq_in, 16)
            sp.dma_start(wk_raw[:], wk).then_inc(wk_in, 16)
            sp.dma_start(x_raw[:], x[0]).then_inc(x_in, 16)
            sp.dma_start(mask_raw[:], mask[0]).then_inc(mask_in, 16)
            sp.dma_start(bk_sb[:], bk).then_inc(bias_in, 16)
            sp.dma_start(wv_raw[:], wv).then_inc(wv_in, 16)
            sp.dma_start(bv_sb[:], bv).then_inc(bias_in, 16)
            sp.dma_start(b1_sb[:], b1).then_inc(bias_in, 16)
            sp.dma_start(bo_sb[:], bo.to_broadcast([P, DM])).then_inc(bias_in, 16)
            sp.dma_start(b2_sb[:], b2.to_broadcast([P, DM])).then_inc(bias_in, 16)
            with sp.Fori(1, CHUNKS) as c:
                sp.wait_ge(mt_in, 16)
                sp.wait_ge(xhi_ready, c)
                sp.wait_ge(xlo_ready, c)
                sp.wait_ge(lower_ready, c * QT)
                sp.dma_start(x_raw[:], x[bass.ds(c, 1)].rearrange("a p k n -> (a p) k n")).then_inc(x_in, 16)
                sp.dma_start(mask_raw[:], mask[bass.ds(c, 1)].rearrange("a p k n -> (a p) k n")).then_inc(mask_in, 16)
            sp.wait_ge(stats_kept, 2 * CHUNKS * PAIRS)
            sp.wait_ge(tp_copied[2], CHUNKS * PAIRS * TP_USES)
            sp.dma_start(wo_raw[:], wo).then_inc(wo_in, 16)
            sp.dma_start(m_res[:], mn).then_inc(mres_in, 16)
            for j in range(2):
                sp.dma_start(w1_raw[:, j], w1[j]).then_inc(w1_in[j], 16)
                sp.dma_start(w2_raw[:, j], w2[j]).then_inc(w2_in[j], 16)
            with sp.Fori(2, FT - 1, 2) as i:
                for j in range(2):
                    for taken in (w1hi, w1lo, w2hi, w2lo):
                        sp.wait_ge(taken, i - 1 + j)
                    sp.dma_start(w1_raw[:, j], w1[bass.ds(i + j, 1)].rearrange("a p k n -> (a p) k n")).then_inc(w1_in[j], 16)
                    sp.dma_start(w2_raw[:, j], w2[bass.ds(i + j, 1)].rearrange("a p n -> (a p) n")).then_inc(w2_in[j], 16)
            for t in range(QT):
                sp.wait_ge(z_ready, t + 1)
                sp.dma_start(out[t], norm[:, t]).then_inc(out_done, 16)
            sp.wait_ge(out_done, 16 * QT)

        @block.gpsimd
        def _(pool):
            nc.gpsimd.memset(ident[:], 0.0).then_inc(zeroed, 1)
            nc.gpsimd.memset(total[:], 0.0)
            nc.gpsimd.memset(acc[:], 0.0)
            nc.gpsimd.memset(negmax_old[:], 3e38).then_inc(zeroed, 1)
            pool.wait_ge(zeroed, 2)
            nc.gpsimd.affine_select(out=ident[:], in_=ident[:], compare_op=ALU.not_equal, fill=1.0, base=0,
                                    pattern=[[-1, P]], channel_multiplier=1).then_inc(ident_ready, 1)

            def lower_tile(t):
                nc.gpsimd.tensor_scalar(lower[:, t], mask_raw[:, t], -1.0, -BIG, ALU.add, ALU.mult).then_inc(lower_ready, 1)

            pool.wait_ge(x_in, 16)
            pool.wait_ge(xhi_ready, 1)
            nc.gpsimd.tensor_tensor(x2[1][:], x_raw[:], x2[0][:], ALU.subtract).then_inc(xlo_ready, 1)
            pool.wait_ge(mask_in, 16)
            for t in range(QT):
                lower_tile(t)
            pool.wait_ge(wv_hi, 1)
            nc.gpsimd.tensor_tensor(wv2[1][:], wv_raw[:], wv2[0][:], ALU.subtract).then_inc(wv_lo, 1)

            def body(c, sched):
                plan = slot_plan(sched)
                if isinstance(c, int) and c == CHUNKS - 1:
                    pool.wait_ge(lower_ready, CHUNKS * QT)
                    nc.gpsimd.memset(lower[:, :, N - c * CHUNK:], 2 * BIG).then_inc(lower_ready, 1)
                for step in sched:
                    kind, p, i = step
                    if kind == "Z":
                        n, p = pair_no(c, p), p % PAIRS
                        pool.wait_ge(exp_done, n * U + U)
                        nc.gpsimd.tensor_tensor(drop[:, p], negmax[:, p], negmax_old[:, p], ALU.subtract).then_inc(drop_ready, 1)
                        read = in_register(pool, n + 1)
                        pool.wait_ge(zeroed, 2)
                        pool.wait_ge(drop_ready, read)
                        nc.gpsimd.tensor_copy(negmax_old[:, p], negmax[:, p]).then_inc(stats_kept, 1)
                        pool.wait_ge(alpha_ready, n + 1)
                        nc.gpsimd.tensor_tensor(total[:, p], total[:, p], alpha[:, p], ALU.mult).then_inc(total_scaled, 1)
                        pool.wait_ge(total_scaled, n + 1)
                        nc.gpsimd.tensor_tensor(total[:, p], total[:, p], psumrow[:, p], ALU.add).then_inc(stats_kept, 1)
                        if not isinstance(n, int) or n >= PAIRS:
                            pool.wait_ge(tp_copied[2], (n - PAIRS + 1) * TP_USES + 1)
                        nc.gpsimd.tensor_tensor(by_head(acc[:, p]), by_head(acc[:, p]), per_head(alpha, p), ALU.mult).then_inc(acc_scaled, 1)
                    if kind == "X":
                        j, before = slot_use(c, plan[("V", 0, V_SLOTS - 1)])
                        pool.wait_ge(filled[j], before + 1)
                        pool.wait_ge(xhi_ready, c + 2)
                        nc.gpsimd.tensor_tensor(x2[1][:], x_raw[:], x2[0][:], ALU.subtract).then_inc(xlo_ready, 1)
                if not (isinstance(c, int) and c == CHUNKS - 1):
                    pool.wait_ge(mask_in, 16 * (c + 2))
                    for t in range(QT):
                        j, before = slot_use(c, plan[("S", PAIRS - 1, QT + t)])
                        read = in_register(pool, before + 1)
                        pool.wait_ge(zeroed, 2)
                        pool.wait_ge(drained[j], read)
                        lower_tile(t)

            chunks(pool, body)

            pool.wait_ge(wohi, 1)
            nc.gpsimd.tensor_tensor(wo2[1][:], wo_raw[:], wo2[0][:], ALU.subtract).then_inc(wolo, 1)
            pool.wait_ge(mres_in, 16)
            pool.wait_ge(bias_in, 16 * 5)
            nc.gpsimd.tensor_tensor(m_res[:], m_res[:], bo_sb[:].unsqueeze(1).to_broadcast([P, QT, DM]), ALU.add).then_inc(mres_ready, 1)
            def hidden_lo(i, j):
                pool.wait_ge(hidhi, i + j + 1)
                nc.gpsimd.tensor_tensor(hid2[1][:, j], hid[:, j], hid2[0][:, j], ALU.subtract).then_inc(hidlo, 1)

            def inv_deviation(t, before):
                pool.wait_ge(var_ready, before + t + 1)
                nc.gpsimd.tensor_scalar(var_eps[:, t:t + 1], meanvar[:, t, 1:2], EPS, None, ALU.add).then_inc(var_kept, 1)
                pool.wait_ge(var_kept, before + t + 1)
                nc.gpsimd.tensor_tensor(rstd[:, t:t + 1], var_eps[:, t:t + 1], minus_half[:], ALU.pow).then_inc(rstd_ready, 1)

            nc.gpsimd.memset(minus_half[:], -0.5).then_inc(half_ready, 1)
            pool.wait_ge(half_ready, 1)
            for t in range(QT):
                inv_deviation(t, 0)
            for t in range(QT):
                pool.wait_ge(m_ready, t + 1)
                nc.gpsimd.tensor_tensor(m_res[:, t], norm[:, t], b2_sb[:], ALU.add).then_inc(mres2, 1)
            hidden_tiles(pool, hidden_lo)
            for t in range(QT):
                inv_deviation(t, QT)

        @block.scalar
        def _(act):
            act.wait_ge(mt_in, 16)
            nc.scalar.copy(mt2[0][:], mt_raw[:]).then_inc(mt_hi, 1)
            act.wait_ge(wq_in, 16)
            nc.scalar.copy(wq2[0][:], wq_raw[:]).then_inc(wq_hi, 1)
            act.wait_ge(x_in, 16)
            nc.scalar.copy(x2[0][:], x_raw[:]).then_inc(xhi_ready, 1)
            act.wait_ge(wk_in, 16)
            nc.scalar.copy(wk2[0][:], wk_raw[:]).then_inc(wk_hi, 1)
            act.wait_ge(wv_in, 16)
            nc.scalar.copy(wv2[0][:], wv_raw[:]).then_inc(wv_hi, 1)
            for p in range(PAIRS):
                act.wait_ge(filled[p % 2], p // 2 + 1)
                for half, to in HALVES:
                    last = nc.scalar.activation(q2[0][rows(to), 2 * p + half], slot[rows(half), p % 2, 0], ACT.Identity, scale=-SCALE)
                last.then_inc(qhi_done, 1)

            act.wait_ge(bias_in, 16 * 5)

            def keys_hi(p, j, half):
                nc.scalar.activation(kst[rows(half), 2 * p + half].rearrange("p (b n) -> p b n", b=2),
                                     slot[rows(half), j, :, :HALF], ACT.Identity, bias=bk_sb[rows(half), p:p + 1]).then_inc(khi_done, 1)

            for p in range(2):
                g = Q_SLOTS + p
                act.wait_ge(filled[g % 2], g // 2 + 1)
                for half in range(2):
                    keys_hi(p, g % 2, half)

            def body(c, sched):
                plan = slot_plan(sched)
                for step in sched:
                    kind, p, i = step
                    if kind == "E":
                        j, before = slot_use(c, plan[("S", p, i)])
                        act.wait_ge(drained[j], before + 1)
                        unit = prob[:, p % 2, i]
                        nc.scalar.activation(unit, unit, ACT.Exp, bias=negmax[:, p, i:i + 1], scale=-1.0,
                                             accum_out=psumrow[:, p, i:i + 1]).then_inc(exp_done, 1)
                    if kind == "V":
                        j, before = slot_use(c, plan[step])
                        n = min(2, KT - 2 * i)
                        act.wait_ge(filled[j], before + 1)
                        nc.scalar.copy(val[:, 2 * i:2 * i + n], slot[:, j, :n]).then_inc(drained[j], 1)
                    if kind == "H":
                        j, before = slot_use(c, plan[("K", p, 0)])
                        if i == 0:
                            act.wait_ge(filled[j], before + 1)
                        keys_hi(p % PAIRS, j, i)
                    if kind == "T" and i in ACT_COPIES:
                        n = pair_no(c, p) * TV + i
                        b, before = tp_use(pair_no(c, p), i)
                        act.wait_ge(tp_filled[b], before + 1)
                        if not isinstance(n, int) or n >= 4:
                            act.wait_ge(pv_done, n - 3)
                        nc.scalar.copy(pT[:, (p * TV + i) % 4], tp[:, b]).then_inc(tp_copied[b], 1)
                    if kind == "C":
                        n = pair_no(c, p)
                        act.wait_ge(pv_done, (n + 1) * TV)
                        if not isinstance(n, int) or n >= 1:
                            act.wait_ge(tp_filled[2], n * TP_USES)
                        nc.scalar.copy(outT_sb[:], outT[:]).then_inc(outT_copied, 1)
                    if kind == "Z":
                        act.wait_ge(drop_ready, pair_no(c, p) + 1)
                        nc.scalar.activation(alpha[:, p % PAIRS], drop[:, p % PAIRS], ACT.Exp).then_inc(alpha_ready, 1)
                    if kind == "X":
                        j, before = slot_use(c, plan[("V", 0, V_SLOTS - 1)])
                        act.wait_ge(filled[j], before + 1)
                        act.wait_ge(x_in, 16 * (c + 2))
                        nc.scalar.copy(x2[0][:], x_raw[:]).then_inc(xhi_ready, 1)

            chunks(act, body)

            act.wait_ge(wo_in, 16)
            nc.scalar.copy(wo2[0][:], wo_raw[:]).then_inc(wohi, 1)

            def up_weights_hi(n, j):
                act.wait_ge(w1_in[j], (n - j) * 8 + 16)
                nc.scalar.copy(w12[0][:, j], w1_raw[:, j]).then_inc(w1hi, 1)

            def down_weights_hi(n, j):
                act.wait_ge(w2_in[j], (n - j) * 8 + 16)
                nc.scalar.copy(w22[0][:, j], w2_raw[:, j]).then_inc(w2hi, 1)

            for p in range(PAIRS):
                act.wait_ge(aoT_filled, p + 1)
                nc.scalar.activation(ao2[0][:, p], tp[:, p % 2], ACT.Identity, bias=bv_sb[:, p:p + 1]).then_inc(aohi, 1)
            up_weights_hi(0, 0)
            up_weights_hi(1, 1)
            down_weights_hi(0, 0)
            for k in range(MC):
                act.wait_ge(mT_filled, k + 1)
                nc.scalar.copy(mT2[0][:, k], tp[:, k % 2]).then_inc(mThi, 1)

            def hidden_f32(i, j):
                n = i + j
                act.wait_ge(hid_filled, n + 1)
                if not isinstance(n, int) or n >= 2:
                    act.wait_ge(hidlo, n - 1)
                nc.scalar.activation(hid[:, j], tp[:, j], ACT.Relu, bias=b1_sb[:, bass.ds(n, 1)]).then_inc(hid_f32, 1)
                if not isinstance(n, int) or n + 2 < FT:
                    up_weights_hi(n + 2, j)
                if not isinstance(n, int) or n + 1 < FT:
                    if not isinstance(n, int) or n > 0:
                        act.wait_ge(down_done, n)
                    down_weights_hi(n + 1, 1 - j)

            hidden_tiles(act, hidden_f32)

        @block.vector
        def _(dve):
            dve.wait_ge(mt_hi, 1)
            nc.vector.tensor_tensor(mt2[1][:], mt_raw[:], mt2[0][:], ALU.subtract).then_inc(mt_lo, 1)
            dve.wait_ge(wq_hi, 1)
            nc.vector.tensor_tensor(wq2[1][:], wq_raw[:], wq2[0][:], ALU.subtract).then_inc(wq_lo, 1)
            dve.wait_ge(wk_hi, 1)
            nc.vector.tensor_tensor(wk2[1][:], wk_raw[:], wk2[0][:], ALU.subtract).then_inc(wk_lo, 1)
            for p in range(PAIRS):
                dve.wait_ge(qhi_done, p + 1)
                for half, to in HALVES:
                    last = nc.vector.scalar_tensor_tensor(out=q2[1][rows(to), 2 * p + half], in0=slot[rows(half), p % 2, 0],
                                                          scalar=-SCALE, in1=q2[0][rows(half), 2 * p + half],
                                                          op0=ALU.mult, op1=ALU.subtract)
                last.then_inc(drained[p % 2], 1)

            dve.wait_ge(bias_in, 16 * 5)

            def keys_lo(p, j, half):
                lo = nc.vector.scalar_tensor_tensor(
                    out=kst[rows(1 - half), 2 * p + half].rearrange("p (b n) -> p b n", b=2),
                    in0=slot[rows(half), j, :, :HALF], scalar=bk_sb[rows(half), p:p + 1],
                    in1=kst[rows(half), 2 * p + half].rearrange("p (b n) -> p b n", b=2), op0=ALU.add, op1=ALU.subtract)
                if half == 1:
                    lo.then_inc(drained[j], 1)

            for p in range(2):
                g = Q_SLOTS + p
                dve.wait_ge(khi_done, 2 * p + 2)
                for half in range(2):
                    keys_lo(p, g % 2, half)

            dve.wait_ge(zeroed, 2)
            def body(c, sched):
                plan = slot_plan(sched)
                for step in sched:
                    kind, p, i = step
                    if kind == "S":
                        j, before = slot_use(c, plan[step])
                        t = i % QT
                        final = isinstance(c, int) and c == CHUNKS - 1
                        written = in_register(dve, before + 1)
                        masks = taken = None
                        if p == 0 and (i == 0 if final else i < QT):
                            masks = in_register(dve, CHUNKS * QT + 1 if final else c * QT + t + 1)
                        if i == 0 and (not isinstance(c, int) or c > 0):
                            taken = in_register(dve, 2 * (pair_no(c, p) - PAIRS + 1))
                        dve.wait_ge(zeroed, 2)
                        if masks is not None:
                            dve.wait_ge(lower_ready, masks)
                        if taken is not None:
                            dve.wait_ge(stats_kept, taken)
                        dve.wait_ge(filled[j], written)
                        nc.vector.tensor_tensor_reduce(
                            out=prob[:, p % 2, i].rearrange("p (b n) -> p b n", b=2),
                            in0=slot[:, j, :, :HALF], in1=lower[:, t].rearrange("p (b n) -> p b n", b=2),
                            scale=1.0, scalar=negmax_old[:, p, i:i + 1], op0=ALU.add, op1=ALU.min,
                            accum_out=negmax[:, p, i:i + 1]).then_inc(drained[j], 1)
                    if kind == "L":
                        j, before = slot_use(c, plan[("K", p, 0)])
                        dve.wait_ge(khi_done, 2 * (c * PAIRS + p) + 2)
                        keys_lo(p % PAIRS, j, i)
                    if kind == "T" and i not in ACT_COPIES:
                        n = pair_no(c, p) * TV + i
                        b, before = tp_use(pair_no(c, p), i)
                        dve.wait_ge(tp_filled[b], before + 1)
                        if not isinstance(n, int) or n >= 4:
                            dve.wait_ge(pv_done, n - 3)
                        nc.vector.tensor_copy(pT[:, (p * TV + i) % 4], tp[:, b]).then_inc(tp_copied[b], 1)
                    if kind == "A":
                        n = pair_no(c, p)
                        b, before = tp_use(n, TV)
                        dve.wait_ge(acc_scaled, n + 1)
                        dve.wait_ge(tp_filled[b], before + 1)
                        own = acc[:, p % PAIRS].rearrange("p t n -> p (t n)")
                        nc.vector.tensor_tensor(own, own, tp[:, b], ALU.add).then_inc(tp_copied[b], 1)

            chunks(dve, body)

            dve.wait_ge(stats_kept, 2 * CHUNKS * PAIRS)
            dve.wait_ge(tp_copied[2], CHUNKS * PAIRS * TP_USES)
            nc.vector.reciprocal(inv[:], total[:]).then_inc(inv_ready, 1)
            dve.wait_ge(inv_ready, 1)
            for p in range(PAIRS):
                nc.vector.tensor_tensor(by_head(acc[:, p]), by_head(acc[:, p]), per_head(inv, p), ALU.mult).then_inc(norm_ready, 1)
            for p in range(PAIRS):
                dve.wait_ge(aohi, p + 1)
                nc.vector.scalar_tensor_tensor(out=ao2[1][:, p], in0=tp[:, p % 2], scalar=bv_sb[:, p:p + 1], in1=ao2[0][:, p],
                                               op0=ALU.add, op1=ALU.subtract).then_inc(aolo, 1)

            def layer_norm(t, src, count):
                nc.vector.tensor_tensor(norm[:, t], src, m_res[:, t], ALU.add).then_inc(ln_step, 1)
                dve.wait_ge(ln_step, count + 1)
                nc.vector.bn_stats(stats[:, t], norm[:, t]).then_inc(ln_step, 1)
                dve.wait_ge(ln_step, count + 2)
                nc.vector.bn_aggr(meanvar[:, t], stats[:, t]).then_inc(var_ready, 1)

            def layer_scale(t, before, done):
                dve.wait_ge(rstd_ready, before + t + 1)
                nc.vector.tensor_scalar(norm[:, t], norm[:, t], meanvar[:, t, 0:1], rstd[:, t:t + 1],
                                        ALU.subtract, ALU.mult).then_inc(done, 1)

            def up_weights_lo(n, j):
                dve.wait_ge(w1hi, n + 1)
                nc.vector.tensor_tensor(w12[1][:, j], w1_raw[:, j], w12[0][:, j], ALU.subtract).then_inc(w1lo, 1)

            def down_weights_lo(n, j):
                dve.wait_ge(w2hi, n + 1)
                nc.vector.tensor_tensor(w22[1][:, j], w2_raw[:, j], w22[0][:, j], ALU.subtract).then_inc(w2lo, 1)

            dve.wait_ge(mres_ready, 1)
            for t in range(QT):
                dve.wait_ge(proj_done, t + 1)
                layer_norm(t, slot[:, t // 2, t % 2], 2 * t)
                if t >= 1:
                    layer_scale(t - 1, 0, m_ready)
            layer_scale(QT - 1, 0, m_ready)
            up_weights_lo(0, 0)
            up_weights_lo(1, 1)
            down_weights_lo(0, 0)
            for k in range(MC):
                dve.wait_ge(mThi, k + 1)
                nc.vector.tensor_tensor(mT2[1][:, k], tp[:, k % 2], mT2[0][:, k], ALU.subtract).then_inc(mTlo, 1)

            def hidden_hi(i, j):
                n = i + j
                dve.wait_ge(hid_f32, n + 1)
                nc.vector.tensor_copy(hid2[0][:, j], hid[:, j]).then_inc(hidhi, 1)
                if not isinstance(n, int) or n + 2 < FT:
                    up_weights_lo(n + 2, j)
                if not isinstance(n, int) or n + 1 < FT:
                    down_weights_lo(n + 1, 1 - j)

            hidden_tiles(dve, hidden_hi)
            dve.wait_ge(mres2, QT)
            for t in range(QT):
                dve.wait_ge(down_done, FT)
                layer_norm(t, slot[:, t // 2, t % 2], 2 * (QT + t))
                if t >= 1:
                    layer_scale(t - 1, QT, z_ready)
            layer_scale(QT - 1, QT, z_ready)

        @block.tensor
        def _(pe):
            def products(dst, stationary, moving, terms):
                for n, (a, b, k) in enumerate(terms):
                    last = nc.tensor.matmul(dst, stationary(a, k), moving(b, k), start=(n == 0), stop=(n == len(terms) - 1))
                return last

            def split(width):
                return [(a, b, k) for a, b in TERMS for k in range(width)]

            pe.wait_ge(mt_hi, 1)
            pe.wait_ge(wq_hi, 1)
            pe.wait_ge(mt_lo, 1)
            pe.wait_ge(wq_lo, 1)
            for p in range(PAIRS):
                if p >= 2:
                    pe.wait_ge(drained[p % 2], p // 2)
                products(slot[:, p % 2, 0], lambda a, k: wq2[a][:, k, P * p:P * p + P],
                         lambda b, k: mt2[b][:, k], split(MC)).then_inc(filled[p % 2], 1)

            def keys(p, j):
                for b in range(2):
                    last = products(slot[:, j, b, :HALF], lambda a, k: wk2[a][:, k, P * p:P * p + P],
                                    lambda m, k: x2[m][:, k, b * HALF:b * HALF + HALF], split(DC))
                return last

            pe.wait_ge(wk_hi, 1)
            pe.wait_ge(wk_lo, 1)
            pe.wait_ge(xhi_ready, 1)
            pe.wait_ge(xlo_ready, 1)
            for p in range(2):
                g = Q_SLOTS + p
                pe.wait_ge(drained[g % 2], g // 2)
                keys(p, g % 2).then_inc(filled[g % 2], 1)

            pe.wait_ge(wv_hi, 1)
            pe.wait_ge(wv_lo, 1)
            pe.wait_ge(ident_ready, 1)

            def body(c, sched):
                plan = slot_plan(sched)
                for step in sched:
                    kind, p, i = step
                    if step in plan:
                        j, before = slot_use(c, plan[step])
                        pe.wait_ge(drained[j], before)
                    if kind == "S":
                        h, t = 2 * p + i // QT, i % QT
                        for part in range(2):
                            for b in range(2):
                                last = nc.tensor.matmul(slot[:, j, b, :HALF], q2[part][:, h, P * t:P * t + P],
                                                        kst[:, h, b * HALF:b * HALF + HALF], start=(part == 0), stop=(part == 1))
                        last.then_inc(filled[j], 1)
                    if kind == "V":
                        for n in range(min(2, KT - 2 * i)):
                            kt = 2 * i + n
                            last = products(slot[:, j, n], lambda a, k: x2[a][:, k, P * kt:P * kt + P],
                                            lambda m, k: wv2[m][:, k], split(DC))
                        last.then_inc(filled[j], 1)
                    if kind == "K":
                        if p == PAIRS:
                            pe.wait_ge(xhi_ready, c + 2)
                            pe.wait_ge(xlo_ready, c + 2)
                        keys(p % PAIRS, j).then_inc(filled[j], 1)
                    if kind == "T":
                        kt, h = i // 2, i % 2
                        if kt == 0:
                            pe.wait_ge(exp_done, pair_no(c, p) * U + QT * (h + 1))
                        b, before = tp_use(pair_no(c, p), i)
                        if not isinstance(before, int) or before > 0:
                            pe.wait_ge(tp_copied[b], before)
                        for t in range(QT):
                            last = nc.tensor.transpose(tp[:, b, P * t:P * t + P],
                                                       prob[:, p % 2, QT * h + t, P * kt:P * kt + P], ident[:])
                        last.then_inc(tp_filled[b], 1)
                    if kind == "W":
                        kt, h = i // 2, i % 2
                        if i == 0:
                            if p == 0:
                                for v in (V_SLOTS - 2, V_SLOTS - 1):
                                    vj, v_before = slot_use(c, plan[("V", 0, v)])
                                    pe.wait_ge(drained[vj], v_before + 1)
                            if not isinstance(c, int) or pair_no(c, p) > 0:
                                pe.wait_ge(outT_copied, pair_no(c, p))
                        b, before = tp_use(pair_no(c, p), i)
                        pe.wait_ge(tp_copied[b], before + 1)
                        nc.tensor.matmul(outT[DH * h:DH * h + DH], val[:, kt, head(p, h)],
                                         pT[:, (p * TV + i) % 4], start=(kt == 0), stop=(kt == KT - 1)).then_inc(pv_done, 1)
                    if kind == "F":
                        n = pair_no(c, p)
                        b, before = tp_use(n, TV)
                        pe.wait_ge(outT_copied, n + 1)
                        pe.wait_ge(tp_copied[b], before)
                        for t in range(QT):
                            last = nc.tensor.transpose(tp[:, b, P * t:P * t + P], outT_sb[:, P * t:P * t + P], ident[:])
                        last.then_inc(tp_filled[b], 1)

            chunks(pe, body)

            for p in range(PAIRS):
                pe.wait_ge(norm_ready, p + 1)
                if p >= 2:
                    pe.wait_ge(aolo, p - 1)
                for t in range(QT):
                    last = nc.tensor.transpose(tp[:, p % 2, P * t:P * t + P], acc[:, p, t], ident[:])
                last.then_inc(aoT_filled, 1)
            pe.wait_ge(wohi, 1)
            pe.wait_ge(wolo, 1)
            pe.wait_ge(aolo, PAIRS)
            for t in range(QT):
                products(slot[:, t // 2, t % 2], lambda a, k: ao2[a][:, k, P * t:P * t + P],
                         lambda b, k: wo2[b][:, k], split(PAIRS)).then_inc(proj_done, 1)
            pe.wait_ge(m_ready, QT)
            for k in range(MC):
                if k >= 2:
                    pe.wait_ge(mTlo, k - 1)
                for t in range(QT):
                    last = nc.tensor.transpose(tp[:, k % 2, P * t:P * t + P], norm[:, t, P * k:P * k + P], ident[:])
                last.then_inc(mT_filled, 1)

            def up(n, j):
                pe.wait_ge(w1lo, n + 1)
                if not isinstance(n, int) or n >= 2:
                    pe.wait_ge(hid_f32, n - 1)
                products(tp[:, j], lambda a, k: w12[a][:, j, k], lambda b, k: mT2[b][:, k], split(MC)).then_inc(hid_filled, 1)

            def down(n, j, first, last_one):
                pe.wait_ge(w2lo, n + 1)
                pe.wait_ge(hidlo, n + 1)
                for t in range(QT):
                    for i, (a, b) in enumerate(TERMS):
                        last = nc.tensor.matmul(slot[:, t // 2, t % 2], hid2[a][:, j, P * t:P * t + P], w22[b][:, j],
                                                start=first and i == 0, stop=last_one and i == len(TERMS) - 1)
                last.then_inc(down_done, 1)

            pe.wait_ge(mTlo, MC)
            up(0, 0)
            up(1, 1)
            down(0, 0, True, False)
            with pe.Fori(2, FT - 1, 2) as i:
                up(i, 0)
                down(i - 1, 1, False, False)
                up(i + 1, 1)
                down(i, 0, False, False)
            down(FT - 1, 1, False, True)


def layouts(a):
    import numpy as np

    x = np.zeros((NPAD, D), np.float32)
    x[:N] = a["L0_rec_x"]
    mask = np.zeros((E, NPAD), bool)
    mask[:, :N] = a["r_mask"].reshape(E, N)
    m = a["r_M"]
    wkv = a["L0_rec_Wkv"]
    bkv = a["L0_rec_bkv"]

    def rows(w, k):
        return w.T.reshape(k, P, -1).transpose(1, 0, 2)

    return {
        "x": x.reshape(CHUNKS, CHUNK, DC, P).transpose(0, 3, 2, 1),
        "mask": mask.reshape(QT, P, CHUNKS, CHUNK).transpose(2, 1, 0, 3),
        "mt": rows(m, MC),
        "mn": m.reshape(QT, P, DM).transpose(1, 0, 2),
        "wq": rows(a["L0_rec_Wq"], MC),
        "wk": rows(wkv[:INNER], DC),
        "wv": rows(wkv[INNER:], DC),
        "bk": bkv[:INNER].reshape(PAIRS, P).T,
        "bv": bkv[INNER:].reshape(PAIRS, P).T,
        "wo": rows(a["L0_rec_Wo"], PAIRS),
        "bo": a["L0_rec_bo"].reshape(1, DM),
        "w1": a["L0_rec_W1"].reshape(FT, P, MC, P).transpose(0, 3, 2, 1),
        "b1": a["L0_rec_b1"].reshape(FT, P).T,
        "w2": a["L0_rec_W2"].T.reshape(FT, P, DM),
        "b2": a["L0_rec_b2"].reshape(1, DM),
    }


def kernel(**inputs):
    import numpy as np
    import concourse.bacc as bacc
    from concourse.bass_utils import run_bass_kernel_spmd

    arrays = {f"in_{k}": np.ascontiguousarray(v) for k, v in layouts({k: np.asarray(v) for k, v in inputs.items()}).items()}
    nc = bacc.Bacc("TRN2", target_bir_lowering=False, num_devices=1)
    aps = {k[3:]: nc.dram_tensor(k, v.shape, mybir.dt.from_np(v.dtype), kind="ExternalInput").ap() for k, v in arrays.items()}
    out = nc.dram_tensor("out_z", (QT, P, DM), F32, kind="ExternalOutput").ap()
    build(nc, **aps, out=out)
    r = run_bass_kernel_spmd(nc, [arrays], core_ids=[0])
    return r.results[0]["out_z"].reshape(E, DM)
```

```python
from contextlib import ExitStack

import concourse.bass as bass
from concourse import mybir
from concourse.alu_op_type import AluOpType as ALU

ACT = mybir.ActivationFunctionType
F32 = mybir.dt.float32
F32R = mybir.dt.float32r
BF16 = mybir.dt.bfloat16
U8 = mybir.dt.uint8

P = 128
E = 512
N = 6250
D = 256
DM = 512
INNER = 512
HEADS = 8
DH = 64
FF = 2048
QT = E // P
PAIRS = HEADS // 2
U = 2 * QT
KT = 7
CHUNK = KT * P
CHUNKS = -(-N // CHUNK)
NPAD = CHUNKS * CHUNK
HALF = CHUNK // 2
TV = 2 * KT
FT = FF // P
DC = D // P
MC = DM // P
KEYS_AT = 3
BIG = 2.0 ** 100
EPS = 1e-5
SCALE = DH ** -0.5

TERMS = ((0, 0), (0, 1), (1, 0))

V_SLOTS = -(-KT // 2)
PRE = 2
ACT_COPIES = (0, 1, 2, 4, 6, 8, 10, 12)
TP_USES = (TV + 1) // 3
BODY = PAIRS * U + V_SLOTS + PAIRS


def chunk_schedule(first, last):
    out = []

    def products(p, start, keys, ahead):
        done = start
        parts = [[] for _ in range(KT)]
        for n, k in enumerate(keys):
            parts[KEYS_AT + n].extend([("K", k, 0), ("H", k, 0)])
            parts[KEYS_AT + n + 1].append(("H", k, 1))
            parts[KEYS_AT + n + (1 if n + 1 < len(keys) else 2)].extend([("L", k, 0), ("L", k, 1)])
        while ahead < 2:
            out.append(("T", p, ahead))
            ahead += 1
        if p + 1 < PAIRS:
            out.append(("E", p + 1, start - 1))
        for k in range(KT):
            while ahead < min(TV, 2 * k + 4):
                out.append(("T", p, ahead))
                ahead += 1
            if p + 1 == PAIRS and last and k % 2 == 0 and k // 2 < p:
                out.extend([("G", k // 2, 0), ("B", k // 2, 0), ("D", k // 2, 0)])
            if k == 1:
                out.append(("Z", p, 0))
                if p == 0 and not last:
                    out.append(("X", 0, 0))
                if p > 0 and last:
                    out.append(("O", 0, p - 1))
            if p + 1 < PAIRS and done < U:
                for n in range(2):
                    if done < U:
                        out.extend([("S", p + 1, done)])
                        if done > start:
                            out.append(("E", p + 1, done - 1))
                        done += 1
                    if k == 0 and n == 0:
                        out.extend([("W", p, 0), ("W", p, 1)])
            elif p + 1 < PAIRS and k == KEYS_AT:
                out.append(("E", p + 1, U - 1))
            out.extend(parts[k])
            if ("W", p, 2 * k) not in out:
                out.extend([("W", p, 2 * k), ("W", p, 2 * k + 1)])

    def output(p):
        return [] if first and p < 0 else [("F", p, 0), ("A", p, 0)] + ([("N", p, 0)] if last and p >= 0 else [])

    for p in range(PAIRS):
        keys = (2, 3) if p == 0 else () if p == 1 or last else (PAIRS + p - 2,)
        copy = [] if first and p <= 1 else [("C", p - 2, 0)]
        if p == 1 and not first:
            out.extend([*copy, ("V", 0, 0), ("S", 1, 0), ("T", 0, 0),
                        ("V", 0, 1), *output(-1), ("S", 1, 1), ("E", 1, 0), ("T", 0, 1),
                        ("V", 0, 2), ("S", 1, 2), ("T", 0, 2), ("V", 0, 3), ("E", 1, 1), ("S", 1, 3), ("E", 1, 2)])
            products(0, 4, keys, 3)
            continue
        if first and p == 0:
            for i in range(U):
                out.extend([("S", 0, i)] + ([("V", 0, i // 2)] if i % 2 == 0 else []) + ([("E", 0, i - 1)] if i else []))
                if i in (1, 3):
                    k = keys[i // 2]
                    out.extend([("K", k, 0), ("H", k, 0), ("H", k, 1)])
                if i in (3, 6):
                    k = keys[i // 4]
                    out.extend([("L", k, 0), ("L", k, 1)])
            out.append(("E", 0, U - 1))
            continue
        out.extend([("S", p, 0), *copy, *output(p - 2), ("S", p, 1)])
        if first and p == 1:
            out.extend([("T", 0, 0), ("T", 0, 1), ("E", 1, 0)])
            products(0, 2, keys, 2)
        else:
            out.extend([("T", p - 1, 0), ("T", p - 1, 1), ("E", p, 0)])
            products(p - 1, 2, keys, 2)
    if last:
        tail = PAIRS - 1
        out.extend([("C", tail - 1, 0), ("T", tail, 0), ("T", tail, 1), *output(tail - 1)])
        products(tail, U, (), 2)
        out.extend([("C", tail, 0), ("Y", 0, 0), *output(tail), ("Y", 0, 1), ("G", tail, 0), ("B", tail, 0), ("D", tail, 0),
                    ("Y", 0, 2), ("R", 0, 0), ("R", 0, 1), ("R", 0, 2), ("Y", 0, 3), ("R", 0, 3)])
    return out


def build(nc, x, mask, mt, mn, wq, wk, wv, bk, bv, wo, bo, w1, b1, w2, b2, out):
    with ExitStack() as ctx:
        def sb(name, shape, dt, where=ctx):
            return where.enter_context(nc.sbuf_tensor(name, shape, dt))

        def psum(name, shape):
            return ctx.enter_context(nc.psum_tensor(name, shape, F32))

        def sem(name):
            return ctx.enter_context(nc.semaphore(name))

        slot = psum("slot", [P, 2, 2, 512])
        tail = psum("tail", [P, 4, 512])
        tp = tail[:, :3]
        outT = tail[:, 3]

        ident = sb("ident", [P, P], F32)
        q2 = [sb("q2_hi", [P, HEADS, E], F32R), sb("q2_lo", [P, HEADS, E], F32R)]
        acc = sb("acc", [P, PAIRS, QT, P], F32)
        bk_sb = sb("bk_sb", [P, PAIRS], F32)
        bv_sb = sb("bv_sb", [P, PAIRS], F32)
        b1_sb = sb("b1_sb", [P, FT], F32)
        bo_sb = sb("bo_sb", [P, DM], F32)
        b2_sb = sb("b2_sb", [P, DM], F32)
        negmax_old = sb("negmax_old", [P, PAIRS, U], F32)
        negmax = sb("negmax", [P, PAIRS, U], F32)
        drop = sb("drop", [P, PAIRS, U], F32)
        alpha = sb("alpha", [P, PAIRS, U], F32)
        psumrow = sb("psumrow", [P, PAIRS, U], F32)
        total = sb("total", [P, PAIRS, U], F32)
        inv = sb("inv", [P, PAIRS, U], F32)
        minus_half = sb("minus_half", [P, 1], F32)

        att = ctx.enter_context(ExitStack())
        wk2 = [sb("wk_hi", [P, DC, INNER], F32R, att), sb("wk_lo", [P, DC, INNER], F32R, att)]
        wv2 = [sb("wv_hi", [P, DC, INNER], F32R, att), sb("wv_lo", [P, DC, INNER], F32R, att)]
        x_raw = sb("x_raw", [P, DC, CHUNK], F32, att)
        x2 = [sb("x_hi", [P, DC, CHUNK], F32R, att), sb("x_lo", [P, DC, CHUNK], F32R, att)]
        mask_raw = sb("mask_raw", [P, QT, CHUNK], U8, att)
        kst = sb("kst", [P, HEADS, CHUNK], F32R, att)
        val = sb("val", [P, KT, INNER], F32, att)
        lower = sb("lower", [P, QT, CHUNK], BF16, att)
        pT = sb("pT", [P, 4, E], F32, att)
        outT_sb = sb("outT_sb", [P, E], F32, att)
        pro = att.enter_context(ExitStack())
        prob = sb("prob", [P, 2, U, CHUNK], F32, pro)
        pro.close()
        pre = att.enter_context(ExitStack())
        mt_raw = sb("mt_raw", [P, MC, E], F32, pre)
        wq_raw = sb("wq_raw", [P, MC, INNER], F32, pre)
        mt2 = [sb("mt_hi", [P, MC, E], F32R, pre), sb("mt_lo", [P, MC, E], F32R, pre)]
        wq2 = [sb("wq_hi", [P, MC, INNER], F32R, pre), sb("wq_lo", [P, MC, INNER], F32R, pre)]
        wk_raw = sb("wk_raw", [P, DC, INNER], F32, pre)
        wv_raw = sb("wv_raw", [P, DC, INNER], F32, pre)
        pre.close()
        att.close()

        wo_raw = sb("wo_raw", [P, PAIRS, DM], F32)
        wo2 = [sb("wo_hi", [P, PAIRS, DM], F32R), sb("wo_lo", [P, PAIRS, DM], F32R)]
        m_res = sb("m_res", [P, QT, DM], F32)
        w1_raw = sb("w1_raw", [P, 2, MC, P], F32)
        w2_raw = sb("w2_raw", [P, 2, DM], F32)
        ao2 = [sb("ao_hi", [P, PAIRS, E], F32R), sb("ao_lo", [P, PAIRS, E], F32R)]
        w12 = [sb("w1_hi", [P, 2, MC, P], F32R), sb("w1_lo", [P, 2, MC, P], F32R)]
        w22 = [sb("w2_hi", [P, 2, DM], F32R), sb("w2_lo", [P, 2, DM], F32R)]
        norm = sb("norm", [P, QT, DM], F32)
        stats = sb("stats", [P, QT, 6], F32)
        meanvar = sb("meanvar", [P, QT, 2], F32)
        var_eps = sb("var_eps", [P, QT], F32)
        rstd = sb("rstd", [P, QT], F32)
        shift = sb("shift", [P, QT], F32)
        mT2 = [sb("mT_hi", [P, MC, E], F32R), sb("mT_lo", [P, MC, E], F32R)]
        hid = sb("hid", [P, 2, E], F32)
        hid2 = [sb("hid_hi", [P, 2, E], F32R), sb("hid_lo", [P, 2, E], F32R)]

        wk_in, wv_in = sem("wk_in"), sem("wv_in")
        mt_in, wq_in, x0_in = [[sem(f"{name}_in{i}") for i in range(2)] for name in ("mt", "wq", "x0")]
        x_in, mask_in, bk_in, bias_in = sem("x_in"), sem("mask_in"), sem("bk_in"), sem("bias_in")
        wo_in, mres_in = sem("wo_in"), sem("mres_in")
        w1_in, w2_in = [sem("w1_in0"), sem("w1_in1")], [sem("w2_in0"), sem("w2_in1")]
        out_done = sem("out_done")
        zeroed, ident_ready = sem("zeroed"), sem("ident_ready")
        mt_hi, wq_hi, wk_hi, wv_hi = sem("mt_hi_s"), sem("wq_hi_s"), sem("wk_hi_s"), sem("wv_hi_s")
        mt_lo, wq_lo, wk_lo, wv_lo = sem("mt_lo_s"), sem("wq_lo_s"), sem("wk_lo_s"), sem("wv_lo_s")
        xhi_ready, xlo_ready = sem("xhi_ready"), sem("xlo_ready")
        filled = [sem("filled0"), sem("filled1")]
        drained = [sem("drained0"), sem("drained1")]
        q_filled, early_filled, early_placed = sem("q_filled"), sem("early_filled"), sem("early_placed")
        qhi_done, qlo_done, khi_done = sem("qhi_done"), sem("qlo_done"), sem("khi_done")
        q_placed = [sem(f"q_placed{p}") for p in range(PAIRS)]
        lower_ready = sem("lower_ready")
        exp_done = sem("exp_done")
        tp_filled = [sem(f"tp_filled{b}") for b in range(3)]
        tp_copied = [sem(f"tp_copied{b}") for b in range(3)]
        pv_done = sem("pv_done")
        outT_copied = sem("outT_copied")
        acc_scaled = sem("acc_scaled")
        drop_ready, alpha_ready = sem("drop_ready"), sem("alpha_ready")
        total_scaled, stats_kept = sem("total_scaled"), sem("stats_kept")
        inv_ready, norm_ready = sem("inv_ready"), sem("norm_ready")
        aoT_filled, aohi, aolo = sem("aoT_filled"), sem("aohi_s"), sem("aolo_s")
        wohi, wolo, mres_ready = sem("wohi_s"), sem("wolo_s"), sem("mres_ready")
        proj_done, m_ready, ln_step, mres2 = sem("proj_done"), sem("m_ready"), sem("ln_step"), sem("mres2")
        mT_filled, mThi, mTlo = sem("mT_filled"), sem("mThi_s"), sem("mTlo_s")
        w1hi, w1lo, w2hi, w2lo = sem("w1hi_s"), sem("w1lo_s"), sem("w2hi_s"), sem("w2lo_s")
        hid_filled, hidhi, hid_f32, hidlo = sem("hid_filled"), sem("hidhi_s"), sem("hid_f32"), sem("hidlo_s")
        shift_ready, var_kept = sem("shift_ready"), sem("var_kept")
        var_ready, rstd_ready = sem("var_ready"), sem("rstd_ready")
        down_done, z_ready = sem("down_done"), sem("z_ready")

        def in_register(eng, value):
            return value if isinstance(value, int) else eng.to_reg(value)

        def rows(half):
            return slice(DH * half, DH * half + DH)

        def x_taken(c):
            return c + 2

        def q_bank(p):
            return tail[:, p]

        def early(c, p):
            return isinstance(c, int) and c == 0 and 2 <= p < PAIRS

        def key_banks(c, p, j):
            return tail[:, 2 * p - PAIRS:2 * p - PAIRS + 2, :HALF] if early(c, p) else slot[:, j, :, :HALF]

        def slot_use(c, i):
            g = PRE + i if isinstance(c, int) and c == 0 else i
            return g % 2, c * (BODY // 2) + g // 2

        def slot_plan(c, sched):
            plan, i = {}, 0
            for step in sched:
                if step[0] in "SV" or step[0] == "K" and not early(c, step[1]):
                    plan[step] = i
                    i += 1
            return plan

        def pair_no(c, p):
            return c * PAIRS + p

        def tp_use(n, i):
            return i % 3, n * TP_USES + i // 3

        def chunks(eng, body):
            body(0, chunk_schedule(True, False))
            mid = chunk_schedule(False, False)
            with eng.Fori(1, CHUNKS - 1) as c:
                body(c, mid)
            body(CHUNKS - 1, chunk_schedule(False, True))

        def hidden_tiles(eng, body):
            for j in range(2):
                body(0, j)
            with eng.Fori(2, FT - 3, 2) as i:
                for j in range(2):
                    body(i, j)
            for j in range(2):
                body(FT - 2, j)

        def per_head(stat, p):
            v = stat[:, p, :].rearrange("p (h t) -> p t h", h=2)
            return v.unsqueeze(3).to_broadcast([P, QT, 2, DH])

        def head(p, h):
            start = P * (p % PAIRS) + DH * h
            return slice(start, start + DH)

        def m_bank(t):
            return tail[:, 1 + t % 3].rearrange("p (k n) -> p k n", k=MC)

        def gather_bank(p):
            return tp[:, 0] if p == PAIRS - 1 else slot[:, p // 2, p % 2]

        def by_head(t):
            return t.rearrange("p t (h d) -> p t h d", h=2)

        block = ctx.enter_context(nc.Block())

        @block.sync
        def _(sp):
            sp.dma_start(wk_raw[:], wk).then_inc(wk_in, 16)
            for b in range(2):
                cols = slice(b * HALF, b * HALF + HALF)
                sp.dma_start(x_raw[:, :, cols], x[0, :, :, cols]).then_inc(x0_in[b], 16)
            for i in range(2):
                part = slice(i * MC // 2, (i + 1) * MC // 2)
                sp.dma_start(mt_raw[:, part], mt[:, part]).then_inc(mt_in[i], 16)
                sp.dma_start(wq_raw[:, part], wq[:, part]).then_inc(wq_in[i], 16)
            sp.dma_start(bk_sb[:], bk).then_inc(bk_in, 16)
            sp.dma_start(mask_raw[:], mask[0]).then_inc(mask_in, 16)
            sp.dma_start(wv_raw[:], wv).then_inc(wv_in, 16)
            sp.dma_start(bv_sb[:], bv).then_inc(bias_in, 16)
            sp.dma_start(b1_sb[:], b1).then_inc(bias_in, 16)
            sp.dma_start(bo_sb[:], bo.to_broadcast([P, DM])).then_inc(bias_in, 16)
            sp.dma_start(b2_sb[:], b2.to_broadcast([P, DM])).then_inc(bias_in, 16)
            for p in range(PAIRS):
                for part, done in enumerate((qhi_done, qlo_done)):
                    sp.wait_ge(done, p + 1)
                    for half in range(2):
                        sp.dma_start(q2[part][rows(1 - half), 2 * p + half].bitcast(F32),
                                     q2[part][rows(half), 2 * p + half].bitcast(F32)).then_inc(q_placed[p], 16)
            with sp.Fori(1, CHUNKS) as c:
                taken, lowered = in_register(sp, x_taken(c - 1)), in_register(sp, c * QT)
                sp.wait_ge(wk_in, 16)
                sp.wait_ge(xhi_ready, taken)
                sp.wait_ge(xlo_ready, taken)
                sp.wait_ge(lower_ready, lowered)
                sp.dma_start(x_raw[:], x[bass.ds(c, 1)].rearrange("a p k n -> (a p) k n")).then_inc(x_in, 16)
                sp.dma_start(mask_raw[:], mask[bass.ds(c, 1)].rearrange("a p k n -> (a p) k n")).then_inc(mask_in, 16)
            j, before = slot_use(CHUNKS - 1, slot_plan(CHUNKS - 1, chunk_schedule(False, True))[("V", 0, V_SLOTS - 1)])
            sp.wait_ge(filled[j], before + 1)
            sp.wait_ge(lower_ready, CHUNKS * QT)
            sp.dma_start(wo_raw[:], wo).then_inc(wo_in, 16)
            sp.dma_start(m_res[:], mn).then_inc(mres_in, 16)
            for j in range(2):
                sp.dma_start(w1_raw[:, j], w1[j]).then_inc(w1_in[j], 16)
                sp.dma_start(w2_raw[:, j], w2[j]).then_inc(w2_in[j], 16)
            with sp.Fori(2, FT - 1, 2) as i:
                for j in range(2):
                    for taken in (w1hi, w1lo, w2hi, w2lo):
                        sp.wait_ge(taken, i - 1 + j)
                    sp.dma_start(w1_raw[:, j], w1[bass.ds(i + j, 1)].rearrange("a p k n -> (a p) k n")).then_inc(w1_in[j], 16)
                    sp.dma_start(w2_raw[:, j], w2[bass.ds(i + j, 1)].rearrange("a p n -> (a p) n")).then_inc(w2_in[j], 16)
            for t in range(QT):
                sp.wait_ge(z_ready, t + 1)
                sp.dma_start(out[t], norm[:, t]).then_inc(out_done, 16)
            sp.wait_ge(out_done, 16 * QT)

        @block.gpsimd
        def _(pool):
            nc.gpsimd.memset(ident[:], 0.0).then_inc(zeroed, 1)
            nc.gpsimd.memset(total[:], 0.0)
            nc.gpsimd.memset(minus_half[:], -0.5)
            nc.gpsimd.memset(acc[:], 0.0)
            nc.gpsimd.memset(negmax_old[:], 3e38).then_inc(zeroed, 1)
            pool.wait_ge(zeroed, 2)
            nc.gpsimd.affine_select(out=ident[:], in_=ident[:], compare_op=ALU.not_equal, fill=1.0, base=0,
                                    pattern=[[-1, P]], channel_multiplier=1).then_inc(ident_ready, 1)

            def lower_tile(t):
                nc.gpsimd.tensor_scalar(lower[:, t], mask_raw[:, t], -1.0, -BIG, ALU.add, ALU.mult).then_inc(lower_ready, 1)

            pool.wait_ge(mask_in, 16)
            for t in range(2):
                lower_tile(t)
            pool.wait_ge(wv_hi, 1)
            nc.gpsimd.tensor_tensor(wv2[1][:], wv_raw[:], wv2[0][:], ALU.subtract).then_inc(wv_lo, 1)
            for t in range(2, QT):
                lower_tile(t)

            def body(c, sched):
                plan = slot_plan(c, sched)
                if isinstance(c, int) and c == CHUNKS - 1:
                    pool.wait_ge(lower_ready, CHUNKS * QT)
                    nc.gpsimd.memset(lower[:, :, N - c * CHUNK:], 2 * BIG).then_inc(lower_ready, 1)
                for step in sched:
                    kind, p, i = step
                    if kind == "Z":
                        n, p = pair_no(c, p), p % PAIRS
                        pool.wait_ge(exp_done, n * U + U)
                        nc.gpsimd.tensor_tensor(drop[:, p], negmax[:, p], negmax_old[:, p], ALU.subtract).then_inc(drop_ready, 1)
                        read = in_register(pool, n + 1)
                        pool.wait_ge(zeroed, 2)
                        pool.wait_ge(drop_ready, read)
                        nc.gpsimd.tensor_copy(negmax_old[:, p], negmax[:, p]).then_inc(stats_kept, 1)
                        pool.wait_ge(alpha_ready, n + 1)
                        nc.gpsimd.tensor_tensor(total[:, p], total[:, p], alpha[:, p], ALU.mult).then_inc(total_scaled, 1)
                        pool.wait_ge(total_scaled, n + 1)
                        nc.gpsimd.tensor_tensor(total[:, p], total[:, p], psumrow[:, p], ALU.add).then_inc(stats_kept, 1)
                        if not isinstance(n, int) or n >= PAIRS:
                            pool.wait_ge(tp_copied[2], (n - PAIRS + 1) * TP_USES + 1)
                        nc.gpsimd.tensor_tensor(by_head(acc[:, p]), by_head(acc[:, p]), per_head(alpha, p), ALU.mult).then_inc(acc_scaled, 1)
                    if kind == "O" and i == 0:
                        pool.wait_ge(wo_in, 16)
                        nc.gpsimd.tensor_copy(wo2[0][:], wo_raw[:]).then_inc(wohi, 1)
                    if kind == "O" and i == 1:
                        pool.wait_ge(wohi, 1)
                        nc.gpsimd.tensor_tensor(wo2[1][:], wo_raw[:], wo2[0][:], ALU.subtract).then_inc(wolo, 1)
                    if kind == "O" and i == 2:
                        pool.wait_ge(mres_in, 16)
                        pool.wait_ge(bias_in, 16 * 4)
                        nc.gpsimd.tensor_tensor(m_res[:], m_res[:], bo_sb[:].unsqueeze(1).to_broadcast([P, QT, DM]), ALU.add).then_inc(mres_ready, 1)
                    if kind == "X":
                        j, before = slot_use(c, plan[("V", 0, V_SLOTS - 1)])
                        read, loaded, taken = [in_register(pool, v) for v in (before + 1, 16 * (c + 1), x_taken(c + 1))]
                        pool.wait_ge(zeroed, 2)
                        pool.wait_ge(filled[j], read)
                        pool.wait_ge(x_in, loaded)
                        nc.gpsimd.tensor_copy(x2[0][:], x_raw[:]).then_inc(xhi_ready, 1)
                        pool.wait_ge(xhi_ready, taken)
                        nc.gpsimd.tensor_tensor(x2[1][:], x_raw[:], x2[0][:], ALU.subtract).then_inc(xlo_ready, 1)
                if not (isinstance(c, int) and c == CHUNKS - 1):
                    pool.wait_ge(mask_in, 16 * (c + 2))
                    for t in range(QT):
                        j, before = slot_use(c, plan[("S", PAIRS - 1, QT + t)])
                        read = in_register(pool, before + 1)
                        pool.wait_ge(zeroed, 2)
                        pool.wait_ge(drained[j], read)
                        lower_tile(t)

            chunks(pool, body)

            def hidden_lo(i, j):
                pool.wait_ge(hidhi, i + j + 1)
                nc.gpsimd.tensor_tensor(hid2[1][:, j], hid[:, j], hid2[0][:, j], ALU.subtract).then_inc(hidlo, 1)

            def inv_deviation(t, before):
                pool.wait_ge(var_ready, before + t + 1)
                nc.gpsimd.tensor_scalar(var_eps[:, t:t + 1], meanvar[:, t, 1:2], EPS, None, ALU.add).then_inc(var_kept, 1)
                pool.wait_ge(var_kept, before + t + 1)
                nc.gpsimd.tensor_tensor(rstd[:, t:t + 1], var_eps[:, t:t + 1], minus_half[:], ALU.pow).then_inc(rstd_ready, 1)
                pool.wait_ge(rstd_ready, before + t + 1)
                nc.gpsimd.tensor_scalar(shift[:, t:t + 1], meanvar[:, t, 0:1], rstd[:, t:t + 1], -1.0, ALU.mult, ALU.mult).then_inc(shift_ready, 1)

            for t in range(QT):
                inv_deviation(t, 0)
            for t in range(QT):
                pool.wait_ge(m_ready, t + 1)
                nc.gpsimd.tensor_tensor(m_res[:, t], norm[:, t], b2_sb[:], ALU.add).then_inc(mres2, 1)
            hidden_tiles(pool, hidden_lo)
            for t in range(QT):
                inv_deviation(t, QT)

        @block.scalar
        def _(act):
            def keys_hi(p, banks, half):
                nc.scalar.activation(kst[rows(half), 2 * p + half].rearrange("p (b n) -> p b n", b=2),
                                     banks[rows(half)], ACT.Identity, bias=bk_sb[rows(half), p:p + 1]).then_inc(khi_done, 1)

            act.wait_ge(wk_in, 16)
            nc.scalar.copy(wk2[0][:], wk_raw[:]).then_inc(wk_hi, 1)
            for b in range(2):
                cols = slice(b * HALF, b * HALF + HALF)
                act.wait_ge(x0_in[b], 16)
                nc.scalar.copy(x2[0][:, :, cols], x_raw[:, :, cols]).then_inc(xhi_ready, 1)
            for i in range(2):
                part = slice(i * MC // 2, (i + 1) * MC // 2)
                act.wait_ge(mt_in[i], 16)
                nc.scalar.copy(mt2[0][:, part], mt_raw[:, part]).then_inc(mt_hi, 1)
                act.wait_ge(wq_in[i], 16)
                nc.scalar.copy(wq2[0][:, part], wq_raw[:, part]).then_inc(wq_hi, 1)
            act.wait_ge(bk_in, 16)
            for p in range(2):
                act.wait_ge(filled[p], 1)
                for half in range(2):
                    keys_hi(p, key_banks(None, p, p), half)
            for p in range(PAIRS):
                act.wait_ge(q_filled, p + 1)
                for half in range(2):
                    last = nc.scalar.activation(q2[0][rows(half), 2 * p + half], q_bank(p)[rows(half)], ACT.Identity, scale=-SCALE)
                last.then_inc(qhi_done, 1)
                if p == 0:
                    act.wait_ge(wv_in, 16)
                    nc.scalar.copy(wv2[0][:], wv_raw[:]).then_inc(wv_hi, 1)

            def body(c, sched):
                plan = slot_plan(c, sched)
                for step in sched:
                    kind, p, i = step
                    if kind == "E":
                        j, before = slot_use(c, plan[("S", p, i)])
                        act.wait_ge(drained[j], before + 1)
                        unit = prob[:, p % 2, i]
                        nc.scalar.activation(unit, unit, ACT.Exp, bias=negmax[:, p, i:i + 1], scale=-1.0,
                                             accum_out=psumrow[:, p, i:i + 1]).then_inc(exp_done, 1)
                    if kind == "V":
                        j, before = slot_use(c, plan[step])
                        n = min(2, KT - 2 * i)
                        act.wait_ge(filled[j], before + 1)
                        nc.scalar.copy(val[:, 2 * i:2 * i + n], slot[:, j, :n]).then_inc(drained[j], 1)
                    if kind == "H":
                        j = None
                        if early(c, p):
                            act.wait_ge(early_filled, p - 1)
                        else:
                            j, before = slot_use(c, plan[("K", p, 0)])
                            if i == 0:
                                act.wait_ge(filled[j], before + 1)
                        keys_hi(p % PAIRS, key_banks(c, p, j), i)
                    if kind == "T" and i in ACT_COPIES:
                        n = pair_no(c, p) * TV + i
                        b, before = tp_use(pair_no(c, p), i)
                        act.wait_ge(tp_filled[b], before + 1)
                        if not isinstance(n, int) or n >= 4:
                            act.wait_ge(pv_done, n - 3)
                        nc.scalar.copy(pT[:, (p * TV + i) % 4], tp[:, b]).then_inc(tp_copied[b], 1)
                    if kind == "C":
                        n = pair_no(c, p)
                        act.wait_ge(pv_done, (n + 1) * TV)
                        if not isinstance(n, int) or n >= 1:
                            act.wait_ge(tp_filled[2], n * TP_USES)
                        nc.scalar.copy(outT_sb[:], outT[:]).then_inc(outT_copied, 1)
                    if kind == "B":
                        act.wait_ge(aoT_filled, p + 1)
                        nc.scalar.activation(ao2[0][:, p], gather_bank(p), ACT.Identity, bias=bv_sb[:, p:p + 1]).then_inc(aohi, 1)
                    if kind == "Z":
                        act.wait_ge(drop_ready, pair_no(c, p) + 1)
                        nc.scalar.activation(alpha[:, p % PAIRS], drop[:, p % PAIRS], ACT.Exp).then_inc(alpha_ready, 1)

            chunks(act, body)

            def up_weights_hi(n, j):
                act.wait_ge(w1_in[j], (n - j) * 8 + 16)
                nc.scalar.copy(w12[0][:, j], w1_raw[:, j]).then_inc(w1hi, 1)

            def down_weights_hi(n, j):
                act.wait_ge(w2_in[j], (n - j) * 8 + 16)
                nc.scalar.copy(w22[0][:, j], w2_raw[:, j]).then_inc(w2hi, 1)

            def layer_scale(t, before, done):
                act.wait_ge(shift_ready, before + t + 1)
                nc.scalar.activation(norm[:, t], norm[:, t], ACT.Identity, scale=rstd[:, t:t + 1], bias=shift[:, t:t + 1]).then_inc(done, 1)

            up_weights_hi(0, 0)
            up_weights_hi(1, 1)
            down_weights_hi(0, 0)
            def transposed_hi(t):
                act.wait_ge(mT_filled, t + 1)
                nc.scalar.copy(mT2[0][:, :, P * t:P * t + P], m_bank(t)).then_inc(mThi, 1)

            for t in range(QT):
                layer_scale(t, 0, m_ready)
                if t >= 1:
                    transposed_hi(t - 1)
            transposed_hi(QT - 1)

            def hidden_f32(i, j):
                n = i + j
                act.wait_ge(hid_filled, n + 1)
                if not isinstance(n, int) or n >= 2:
                    act.wait_ge(hidlo, n - 1)
                nc.scalar.activation(hid[:, j], tp[:, j], ACT.Relu, bias=b1_sb[:, bass.ds(n, 1)]).then_inc(hid_f32, 1)
                if not isinstance(n, int) or n + 2 < FT:
                    up_weights_hi(n + 2, j)
                if not isinstance(n, int) or n + 1 < FT:
                    if not isinstance(n, int) or n > 0:
                        act.wait_ge(down_done, n)
                    down_weights_hi(n + 1, 1 - j)

            hidden_tiles(act, hidden_f32)
            for t in range(QT):
                layer_scale(t, QT, z_ready)

        @block.vector
        def _(dve):
            def keys_lo(p, banks, half, done):
                lo = nc.vector.scalar_tensor_tensor(
                    out=kst[rows(1 - half), 2 * p + half].rearrange("p (b n) -> p b n", b=2),
                    in0=banks[rows(half)], scalar=bk_sb[rows(half), p:p + 1],
                    in1=kst[rows(half), 2 * p + half].rearrange("p (b n) -> p b n", b=2), op0=ALU.add, op1=ALU.subtract)
                if half == 1:
                    lo.then_inc(done, 1)

            dve.wait_ge(wk_hi, 1)
            nc.vector.tensor_tensor(wk2[1][:], wk_raw[:], wk2[0][:], ALU.subtract).then_inc(wk_lo, 1)
            for b in range(2):
                cols = slice(b * HALF, b * HALF + HALF)
                dve.wait_ge(xhi_ready, b + 1)
                nc.vector.tensor_tensor(x2[1][:, :, cols], x_raw[:, :, cols], x2[0][:, :, cols], ALU.subtract).then_inc(xlo_ready, 1)
            for i in range(2):
                part = slice(i * MC // 2, (i + 1) * MC // 2)
                dve.wait_ge(mt_hi, i + 1)
                nc.vector.tensor_tensor(mt2[1][:, part], mt_raw[:, part], mt2[0][:, part], ALU.subtract).then_inc(mt_lo, 1)
                dve.wait_ge(wq_hi, i + 1)
                nc.vector.tensor_tensor(wq2[1][:, part], wq_raw[:, part], wq2[0][:, part], ALU.subtract).then_inc(wq_lo, 1)
            dve.wait_ge(bk_in, 16)
            for p in range(2):
                dve.wait_ge(khi_done, 2 * p + 2)
                for half in range(2):
                    keys_lo(p, key_banks(None, p, p), half, drained[p])
            for p in range(PAIRS):
                dve.wait_ge(qhi_done, p + 1)
                for half in range(2):
                    last = nc.vector.scalar_tensor_tensor(out=q2[1][rows(half), 2 * p + half], in0=q_bank(p)[rows(half)],
                                                          scalar=-SCALE, in1=q2[0][rows(half), 2 * p + half],
                                                          op0=ALU.mult, op1=ALU.subtract)
                last.then_inc(qlo_done, 1)

            dve.wait_ge(zeroed, 2)
            def body(c, sched):
                plan = slot_plan(c, sched)
                for step in sched:
                    kind, p, i = step
                    if kind == "S":
                        j, before = slot_use(c, plan[step])
                        t = i % QT
                        final = isinstance(c, int) and c == CHUNKS - 1
                        written = in_register(dve, before + 1)
                        masks = taken = None
                        if p == 0 and (i == 0 if final else i < QT):
                            masks = in_register(dve, CHUNKS * QT + 1 if final else c * QT + t + 1)
                        if i == 0 and (not isinstance(c, int) or c > 0):
                            taken = in_register(dve, 2 * (pair_no(c, p) - PAIRS + 1))
                        dve.wait_ge(zeroed, 2)
                        if masks is not None:
                            dve.wait_ge(lower_ready, masks)
                        if taken is not None:
                            dve.wait_ge(stats_kept, taken)
                        dve.wait_ge(filled[j], written)
                        nc.vector.tensor_tensor_reduce(
                            out=prob[:, p % 2, i].rearrange("p (b n) -> p b n", b=2),
                            in0=slot[:, j, :, :HALF], in1=lower[:, t].rearrange("p (b n) -> p b n", b=2),
                            scale=1.0, scalar=negmax_old[:, p, i:i + 1], op0=ALU.add, op1=ALU.min,
                            accum_out=negmax[:, p, i:i + 1]).then_inc(drained[j], 1)
                    if kind == "L":
                        j = None if early(c, p) else slot_use(c, plan[("K", p, 0)])[0]
                        dve.wait_ge(khi_done, 2 * (c * PAIRS + p) + 2)
                        keys_lo(p % PAIRS, key_banks(c, p, j), i, early_placed if early(c, p) else drained[j])
                    if kind == "T" and i not in ACT_COPIES:
                        n = pair_no(c, p) * TV + i
                        b, before = tp_use(pair_no(c, p), i)
                        dve.wait_ge(tp_filled[b], before + 1)
                        if not isinstance(n, int) or n >= 4:
                            dve.wait_ge(pv_done, n - 3)
                        nc.vector.tensor_copy(pT[:, (p * TV + i) % 4], tp[:, b]).then_inc(tp_copied[b], 1)
                    if kind == "A":
                        n = pair_no(c, p)
                        b, before = tp_use(n, TV)
                        dve.wait_ge(acc_scaled, n + 1)
                        dve.wait_ge(tp_filled[b], before + 1)
                        own = acc[:, p % PAIRS].rearrange("p t n -> p (t n)")
                        nc.vector.tensor_tensor(own, own, tp[:, b], ALU.add).then_inc(tp_copied[b], 1)
                    if kind == "N":
                        n = pair_no(c, p)
                        b, before = tp_use(n, TV)
                        dve.wait_ge(stats_kept, 2 * (n + 1))
                        nc.vector.reciprocal(inv[:, p], total[:, p]).then_inc(inv_ready, 1)
                        dve.wait_ge(tp_copied[b], before + 1)
                        dve.wait_ge(inv_ready, p + 1)
                        nc.vector.tensor_tensor(by_head(acc[:, p]), by_head(acc[:, p]), per_head(inv, p), ALU.mult).then_inc(norm_ready, 1)
                    if kind == "D":
                        dve.wait_ge(aohi, p + 1)
                        nc.vector.scalar_tensor_tensor(out=ao2[1][:, p], in0=gather_bank(p), scalar=bv_sb[:, p:p + 1], in1=ao2[0][:, p],
                                                       op0=ALU.add, op1=ALU.subtract).then_inc(aolo, 1)

            chunks(dve, body)


            def layer_norm(t, src, count):
                nc.vector.tensor_tensor(norm[:, t], src, m_res[:, t], ALU.add).then_inc(ln_step, 1)
                dve.wait_ge(ln_step, count + 1)
                nc.vector.bn_stats(stats[:, t], norm[:, t]).then_inc(ln_step, 1)
                dve.wait_ge(ln_step, count + 2)
                nc.vector.bn_aggr(meanvar[:, t], stats[:, t]).then_inc(var_ready, 1)

            def up_weights_lo(n, j):
                dve.wait_ge(w1hi, n + 1)
                nc.vector.tensor_tensor(w12[1][:, j], w1_raw[:, j], w12[0][:, j], ALU.subtract).then_inc(w1lo, 1)

            def down_weights_lo(n, j):
                dve.wait_ge(w2hi, n + 1)
                nc.vector.tensor_tensor(w22[1][:, j], w2_raw[:, j], w22[0][:, j], ALU.subtract).then_inc(w2lo, 1)

            up_weights_lo(0, 0)
            up_weights_lo(1, 1)
            down_weights_lo(0, 0)

            def transposed_lo(t):
                dve.wait_ge(mThi, t + 1)
                nc.vector.tensor_tensor(mT2[1][:, :, P * t:P * t + P], m_bank(t), mT2[0][:, :, P * t:P * t + P],
                                        ALU.subtract).then_inc(mTlo, 1)

            dve.wait_ge(mres_ready, 1)
            for t in range(QT):
                dve.wait_ge(proj_done, t + 1)
                layer_norm(t, slot[:, t // 2, t % 2], 2 * t)
            for t in range(QT):
                transposed_lo(t)

            def hidden_hi(i, j):
                n = i + j
                dve.wait_ge(hid_f32, n + 1)
                nc.vector.tensor_copy(hid2[0][:, j], hid[:, j]).then_inc(hidhi, 1)
                if not isinstance(n, int) or n + 2 < FT:
                    up_weights_lo(n + 2, j)
                if not isinstance(n, int) or n + 1 < FT:
                    down_weights_lo(n + 1, 1 - j)

            hidden_tiles(dve, hidden_hi)
            dve.wait_ge(mres2, QT)
            for t in range(QT):
                dve.wait_ge(down_done, FT + t)
                layer_norm(t, slot[:, t // 2, t % 2], 2 * (QT + t))

        @block.tensor
        def _(pe):
            def products(dst, stationary, moving, terms):
                for n, (a, b, k) in enumerate(terms):
                    last = nc.tensor.matmul(dst, stationary(a, k), moving(b, k), start=(n == 0), stop=(n == len(terms) - 1))
                return last

            def split(width):
                return [(a, b, k) for a, b in TERMS for k in range(width)]

            def keys_half(p, banks, b):
                return products(banks[:, b], lambda a, k: wk2[a][:, k, P * p:P * p + P],
                                lambda m, k: x2[m][:, k, b * HALF:b * HALF + HALF], split(DC))

            pe.wait_ge(wk_hi, 1)
            pe.wait_ge(wk_lo, 1)
            for b in range(2):
                pe.wait_ge(xhi_ready, b + 1)
                pe.wait_ge(xlo_ready, b + 1)
                for p in range(2):
                    last = keys_half(p, key_banks(None, p, p), b)
                    if b == 1:
                        last.then_inc(filled[p], 1)

            for i in range(2):
                pe.wait_ge(mt_hi, i + 1)
                pe.wait_ge(wq_hi, i + 1)
                pe.wait_ge(mt_lo, i + 1)
                pe.wait_ge(wq_lo, i + 1)
            for p in range(PAIRS):
                products(q_bank(p), lambda a, k: wq2[a][:, k, P * p:P * p + P],
                         lambda b, k: mt2[b][:, k], split(MC)).then_inc(q_filled, 1)

            pe.wait_ge(wv_hi, 1)
            pe.wait_ge(wv_lo, 1)
            pe.wait_ge(ident_ready, 1)

            def project(t, start, end):
                terms = [(a, b, k) for k in range(start, end) for a, b in TERMS]
                for n, (a, b, k) in enumerate(terms):
                    last = nc.tensor.matmul(slot[:, t // 2, t % 2], ao2[a][:, k, P * t:P * t + P], wo2[b][:, k],
                                            start=(start == 0 and n == 0), stop=(end == PAIRS and n == len(terms) - 1))
                return last

            def body(c, sched):
                plan = slot_plan(c, sched)
                for step in sched:
                    kind, p, i = step
                    j = None
                    if step in plan:
                        j, before = slot_use(c, plan[step])
                        pe.wait_ge(drained[j], before)
                    if kind == "S":
                        h, t = 2 * p + i // QT, i % QT
                        if isinstance(c, int) and c == 0 and i == 0:
                            pe.wait_ge(q_placed[p], 16 * 4)
                        for part in range(2):
                            for b in range(2):
                                last = nc.tensor.matmul(slot[:, j, b, :HALF], q2[part][:, h, P * t:P * t + P],
                                                        kst[:, h, b * HALF:b * HALF + HALF], start=(part == 0), stop=(part == 1))
                        last.then_inc(filled[j], 1)
                    if kind == "V":
                        for n in range(min(2, KT - 2 * i)):
                            kt = 2 * i + n
                            last = products(slot[:, j, n], lambda a, k: x2[a][:, k, P * kt:P * kt + P],
                                            lambda m, k: wv2[m][:, k], split(DC))
                        last.then_inc(filled[j], 1)
                    if kind == "K":
                        if p == PAIRS:
                            pe.wait_ge(xhi_ready, x_taken(c + 1))
                            pe.wait_ge(xlo_ready, x_taken(c + 1))
                        if early(c, p):
                            pe.wait_ge(qlo_done, 2 * (p - 1))
                        for b in range(2):
                            last = keys_half(p % PAIRS, key_banks(c, p, j), b)
                        last.then_inc(early_filled if early(c, p) else filled[j], 1)
                    if kind == "T":
                        kt, h = i // 2, i % 2
                        if i == 0 and isinstance(c, int) and c == 0 and p == 0:
                            pe.wait_ge(early_placed, 2)
                        if kt == 0:
                            pe.wait_ge(exp_done, pair_no(c, p) * U + QT * (h + 1))
                        b, before = tp_use(pair_no(c, p), i)
                        if not isinstance(before, int) or before > 0:
                            pe.wait_ge(tp_copied[b], before)
                        for t in range(QT):
                            last = nc.tensor.transpose(tp[:, b, P * t:P * t + P],
                                                       prob[:, p % 2, QT * h + t, P * kt:P * kt + P], ident[:])
                        last.then_inc(tp_filled[b], 1)
                    if kind == "W":
                        kt, h = i // 2, i % 2
                        if i == 0:
                            if p == 0:
                                for v in (V_SLOTS - 2, V_SLOTS - 1):
                                    vj, v_before = slot_use(c, plan[("V", 0, v)])
                                    pe.wait_ge(drained[vj], v_before + 1)
                            if not isinstance(c, int) or pair_no(c, p) > 0:
                                pe.wait_ge(outT_copied, pair_no(c, p))
                        b, before = tp_use(pair_no(c, p), i)
                        pe.wait_ge(tp_copied[b], before + 1)
                        nc.tensor.matmul(outT[DH * h:DH * h + DH], val[:, kt, head(p, h)],
                                         pT[:, (p * TV + i) % 4], start=(kt == 0), stop=(kt == KT - 1)).then_inc(pv_done, 1)
                    if kind == "F":
                        n = pair_no(c, p)
                        b, before = tp_use(n, TV)
                        pe.wait_ge(outT_copied, n + 1)
                        pe.wait_ge(tp_copied[b], before)
                        for t in range(QT):
                            last = nc.tensor.transpose(tp[:, b, P * t:P * t + P], outT_sb[:, P * t:P * t + P], ident[:])
                        last.then_inc(tp_filled[b], 1)

                    if kind == "G":
                        pe.wait_ge(norm_ready, p + 1)
                        if p == 0:
                            for unit in (U - 2, U - 1):
                                gj, g_before = slot_use(c, plan[("S", PAIRS - 1, unit)])
                                pe.wait_ge(drained[gj], g_before + 1)
                        for t in range(QT):
                            last = nc.tensor.transpose(gather_bank(p)[:, P * t:P * t + P], acc[:, p, t], ident[:])
                        last.then_inc(aoT_filled, 1)
                    if kind == "Y":
                        if i == 0:
                            pe.wait_ge(wohi, 1)
                            pe.wait_ge(wolo, 1)
                            pe.wait_ge(aolo, PAIRS - 1)
                        project(i, 0, PAIRS - 1)
                    if kind == "R":
                        pe.wait_ge(aolo, PAIRS)
                        project(i, PAIRS - 1, PAIRS).then_inc(proj_done, 1)

            chunks(pe, body)

            for t in range(QT):
                pe.wait_ge(m_ready, t + 1)
                if t >= 3:
                    pe.wait_ge(mTlo, t - 2)
                for k in range(MC):
                    last = nc.tensor.transpose(m_bank(t)[:, k], norm[:, t, P * k:P * k + P], ident[:])
                last.then_inc(mT_filled, 1)

            def up(n, j):
                pe.wait_ge(w1lo, n + 1)
                if not isinstance(n, int) or n >= 2:
                    pe.wait_ge(hid_f32, n - 1)
                terms = sorted(split(MC), key=lambda term: term[1])
                for i, (a, b, k) in enumerate(terms):
                    if isinstance(n, int) and n == 0 and i in (0, 2 * MC):
                        pe.wait_ge(mTlo if b else mThi, QT)
                    last = nc.tensor.matmul(tp[:, j], w12[a][:, j, k], mT2[b][:, k], start=(i == 0), stop=(i == len(terms) - 1))
                last.then_inc(hid_filled, 1)

            def down(n, j, first, last_one):
                pe.wait_ge(w2lo, n + 1)
                pe.wait_ge(hidlo, n + 1)
                for t in range(QT):
                    for i, (a, b) in enumerate(TERMS):
                        last = nc.tensor.matmul(slot[:, t // 2, t % 2], hid2[a][:, j, P * t:P * t + P], w22[b][:, j],
                                                start=first and i == 0, stop=last_one and i == len(TERMS) - 1)
                    if last_one or t == QT - 1:
                        last.then_inc(down_done, 1)

            up(0, 0)
            up(1, 1)
            down(0, 0, True, False)
            with pe.Fori(2, FT - 1, 2) as i:
                up(i, 0)
                down(i - 1, 1, False, False)
                up(i + 1, 1)
                down(i, 0, False, False)
            down(FT - 1, 1, False, True)


def layouts(a):
    import numpy as np

    x = np.zeros((NPAD, D), np.float32)
    x[:N] = a["L0_rec_x"]
    mask = np.zeros((E, NPAD), bool)
    mask[:, :N] = a["r_mask"].reshape(E, N)
    m = a["r_M"]
    wkv = a["L0_rec_Wkv"]
    bkv = a["L0_rec_bkv"]

    def rows(w, k):
        return w.T.reshape(k, P, -1).transpose(1, 0, 2)

    return {
        "x": x.reshape(CHUNKS, CHUNK, DC, P).transpose(0, 3, 2, 1),
        "mask": mask.reshape(QT, P, CHUNKS, CHUNK).transpose(2, 1, 0, 3),
        "mt": rows(m, MC),
        "mn": m.reshape(QT, P, DM).transpose(1, 0, 2),
        "wq": rows(a["L0_rec_Wq"], MC),
        "wk": rows(wkv[:INNER], DC),
        "wv": rows(wkv[INNER:], DC),
        "bk": bkv[:INNER].reshape(PAIRS, P).T,
        "bv": bkv[INNER:].reshape(PAIRS, P).T,
        "wo": rows(a["L0_rec_Wo"], PAIRS),
        "bo": a["L0_rec_bo"].reshape(1, DM),
        "w1": a["L0_rec_W1"].reshape(FT, P, MC, P).transpose(0, 3, 2, 1),
        "b1": a["L0_rec_b1"].reshape(FT, P).T,
        "w2": a["L0_rec_W2"].T.reshape(FT, P, DM),
        "b2": a["L0_rec_b2"].reshape(1, DM),
    }


def kernel(**inputs):
    import numpy as np
    import concourse.bacc as bacc
    from concourse.bass_utils import run_bass_kernel_spmd

    arrays = {f"in_{k}": np.ascontiguousarray(v) for k, v in layouts({k: np.asarray(v) for k, v in inputs.items()}).items()}
    nc = bacc.Bacc("TRN2", target_bir_lowering=False, num_devices=1)
    aps = {k[3:]: nc.dram_tensor(k, v.shape, mybir.dt.from_np(v.dtype), kind="ExternalInput").ap() for k, v in arrays.items()}
    out = nc.dram_tensor("out_z", (QT, P, DM), F32, kind="ExternalOutput").ap()
    build(nc, **aps, out=out)
    r = run_bass_kernel_spmd(nc, [arrays], core_ids=[0])
    return r.results[0]["out_z"].reshape(E, DM)
```
